# Optimizing a Trainium2 kernel written in Bass

```python
import numpy as np
import jax
import jax.numpy as jnp

def _softmax(x, axis=-1):
    return jax.nn.softmax(x, axis=axis)

def _gelu(x):
    return jax.nn.gelu(x, approximate=True)

def _silu(x):
    return jax.nn.silu(x)

def _sigmoid(x):
    return jax.nn.sigmoid(x)

def _layernorm(x, axis=-1, eps=1e-05):
    m = jnp.mean(x, axis=axis, keepdims=True)
    v = jnp.var(x, axis=axis, keepdims=True)
    return (x - m) / jnp.sqrt(v + eps)

def _scatter_add(tgt, idx, src, axis=0):
    return tgt.at[idx].add(src)

def _segment_sum(src, seg, n):
    return jax.ops.segment_sum(src, seg, n)
kernel_name = 'mk_seq_preln_d1_jaxref_r8_300691'

def setup_inputs(seed: int=0):
    np.random.seed(seed)
    _w = jnp.asarray

    def _L0_attn_setup():
        import jax, jax.numpy as jnp
        import numpy as np
        NUM_HEADS = 16
        D_MODEL = 128
        HEAD_DIM = D_MODEL // NUM_HEADS
        WINDOW = 64
        SCALE = 8.0 / HEAD_DIM
        LN_EPS = 1e-05

        def _layernorm(t, gamma, beta):
            mu = jnp.mean(t, axis=-1, keepdims=True)
            var = jnp.var(t, axis=-1, keepdims=True)
            return (t - mu) * jax.lax.rsqrt(var + LN_EPS) * gamma + beta
        key = jax.random.key(seed)
        ks = jax.random.split(key, 4)
        x = jax.random.normal(ks[0], (4, 1024, D_MODEL), dtype=jnp.float32)
        W_qkv = jax.random.normal(ks[1], (D_MODEL, 3 * D_MODEL), dtype=jnp.float32) * D_MODEL ** (-0.5)
        ln_gamma = jnp.ones((HEAD_DIM,), dtype=jnp.float32)
        ln_beta = jnp.zeros((HEAD_DIM,), dtype=jnp.float32)
        W_proj = jax.random.normal(ks[2], (D_MODEL, D_MODEL), dtype=jnp.float32) * D_MODEL ** (-0.5)
        b_proj = jax.random.normal(ks[3], (D_MODEL,), dtype=jnp.float32) * 0.02
        return {'x': x, 'W_qkv': W_qkv, 'ln_gamma': ln_gamma, 'ln_beta': ln_beta, 'W_proj': W_proj, 'b_proj': b_proj}
    _L0_attn_in = _L0_attn_setup()

    def _L0_ffn_setup():
        import jax, jax.numpy as jnp
        import numpy as np
        DIM = 128
        DEPTH = 6
        HEADS = 16
        DIM_HEAD = 64
        WINDOW = 32
        INNER = HEADS * DIM_HEAD
        DIM_INNER = int(DIM * 4 * 2 / 3)
        QK_SCALE = 8.0

        def shift_tokens(t):
            a, s = jnp.split(t, 2, -1)
            s = jnp.pad(s, ((0, 0), (1, 0), (0, 0)))[:, :-1]
            return jnp.concatenate([a, s], -1)

        def l2norm(t):
            return t / jnp.maximum(jnp.linalg.norm(t, axis=-1, keepdims=True), 1e-12)

        def rotate_half(x):
            x1, x2 = jnp.split(x, 2, -1)
            return jnp.concatenate([-x2, x1], -1)

        def rotary_tables(n):
            half = jnp.arange(0, DIM_HEAD, 2, dtype=jnp.float32)
            inv_freq = 1.0 / 10000.0 ** (half / DIM_HEAD)
            t = jnp.arange(n, dtype=jnp.float32)
            freqs = t[:, None] * inv_freq[None, :]
            freqs = jnp.concatenate([freqs, freqs], -1)
            base_scale = (half + 0.4 * DIM_HEAD) / (1.4 * DIM_HEAD)
            power = (t - n // 2) / (WINDOW // 2)
            scale = base_scale[None, :] ** power[:, None]
            scale = jnp.concatenate([scale, scale], -1)
            return (freqs, scale)

        def local_attention(q, k, v):
            b, h, n, d = q.shape
            w = WINDOW
            nw = n // w
            bq = q.reshape(b, h, nw, w, d)
            bk = k.reshape(b, h, nw, w, d)
            bv = v.reshape(b, h, nw, w, d)

            def look(t):
                p = jnp.pad(t, ((0, 0), (0, 0), (1, 0), (0, 0), (0, 0)))
                return jnp.concatenate([p[:, :, :nw], p[:, :, 1:]], axis=3)
            bk2, bv2 = (look(bk), look(bv))
            seq = jnp.arange(n).reshape(nw, w)
            seq_p = jnp.pad(seq, ((1, 0), (0, 0)), constant_values=-1)
            jt = jnp.concatenate([seq_p[:nw], seq_p[1:]], axis=1)
            it = seq[:, :, None]
            jb = jt[:, None, :]
            mask = (it < jb) | (it > jb + w) | (jb == -1)
            sim = jnp.einsum('bhwie,bhwje->bhwij', bq, bk2) * QK_SCALE
            sim = jnp.where(mask, -jnp.finfo(sim.dtype).max, sim)
            attn = jax.nn.softmax(sim, -1)
            out = jnp.einsum('bhwij,bhwje->bhwie', attn, bv2)
            return out.reshape(b, h, n, d)

        def attn_layer(x, Wqkv, qs, ksc, Wo):
            b, n, _ = x.shape
            qkv = x @ Wqkv
            q, k, v = jnp.split(qkv, 3, -1)
            sh = lambda t: t.reshape(b, n, HEADS, DIM_HEAD).transpose(0, 2, 1, 3)
            q, k, v = (sh(q), sh(k), sh(v))
            q = l2norm(q) * qs
            k = l2norm(k) * ksc
            freqs, scale = rotary_tables(n)
            cos, sin = (jnp.cos(freqs), jnp.sin(freqs))
            q = q * cos * scale + rotate_half(q) * sin * scale
            inv = 1.0 / scale
            k = k * cos * inv + rotate_half(k) * sin * inv
            out = local_attention(q, k, v)
            out = out.transpose(0, 2, 1, 3).reshape(b, n, INNER)
            return out @ Wo

        def ffn_layer(x, g, bln, W1, b1, W2, b2):
            mu = x.mean(-1, keepdims=True)
            var = ((x - mu) ** 2).mean(-1, keepdims=True)
            xn = (x - mu) / jnp.sqrt(var + 1e-05) * g + bln
            hg = xn @ W1 + b1
            a, gate = jnp.split(hg, 2, -1)
            return a * jax.nn.gelu(gate, approximate=False) @ W2 + b2
        key = jax.random.key(seed)
        ks = jax.random.split(key, 8)
        B, N = (2, 256)
        init = lambda k, shape: jax.random.normal(k, shape, jnp.float32) * 0.02
        return {'x': jax.random.normal(ks[0], (B, N, DIM), jnp.float32), 'Wqkv': init(ks[1], (DEPTH, DIM, 3 * INNER)), 'q_scale': jnp.ones((DEPTH, DIM_HEAD), jnp.float32), 'k_scale': jnp.ones((DEPTH, DIM_HEAD), jnp.float32), 'Wo': init(ks[2], (DEPTH, INNER, DIM)), 'ln_g': jnp.ones((DEPTH, DIM), jnp.float32), 'ln_b': jnp.zeros((DEPTH, DIM), jnp.float32), 'W1': init(ks[3], (DEPTH, DIM, 2 * DIM_INNER)), 'b1': jnp.zeros((DEPTH, 2 * DIM_INNER), jnp.float32), 'W2': init(ks[4], (DEPTH, DIM_INNER, DIM)), 'b2': jnp.zeros((DEPTH, DIM), jnp.float32)}
    _L0_ffn_in = _L0_ffn_setup()
    _d = {'L0_attn_x': _L0_attn_in['x'], 'L0_attn_W_qkv': _L0_attn_in['W_qkv'], 'L0_attn_ln_gamma': _L0_attn_in['ln_gamma'], 'L0_attn_ln_beta': _L0_attn_in['ln_beta'], 'L0_attn_W_proj': _L0_attn_in['W_proj'], 'L0_attn_b_proj': _L0_attn_in['b_proj'], 'L0_ffn_Wqkv': _L0_ffn_in['Wqkv'], 'L0_ffn_q_scale': _L0_ffn_in['q_scale'], 'L0_ffn_k_scale': _L0_ffn_in['k_scale'], 'L0_ffn_Wo': _L0_ffn_in['Wo'], 'L0_ffn_ln_g': _L0_ffn_in['ln_g'], 'L0_ffn_ln_b': _L0_ffn_in['ln_b'], 'L0_ffn_W1': _L0_ffn_in['W1'], 'L0_ffn_b1': _L0_ffn_in['b1'], 'L0_ffn_W2': _L0_ffn_in['W2'], 'L0_ffn_b2': _L0_ffn_in['b2']}
    _x0 = _d['L0_attn_x']
    _d['L0_attn_x'] = jax.random.normal(jax.random.fold_in(jax.random.key(seed), 1), (16, 256, 128), dtype=_x0.dtype)
    del _x0
    return _d

def reference(L0_attn_x, L0_attn_W_qkv, L0_attn_ln_gamma, L0_attn_ln_beta, L0_attn_W_proj, L0_attn_b_proj, L0_ffn_Wqkv, L0_ffn_q_scale, L0_ffn_k_scale, L0_ffn_Wo, L0_ffn_ln_g, L0_ffn_ln_b, L0_ffn_W1, L0_ffn_b1, L0_ffn_W2, L0_ffn_b2):

    def _L0_attn_ref(x, W_qkv, ln_gamma, ln_beta, W_proj, b_proj):
        import jax, jax.numpy as jnp
        import numpy as np
        NUM_HEADS = 16
        D_MODEL = 128
        HEAD_DIM = D_MODEL // NUM_HEADS
        WINDOW = 64
        SCALE = 8.0 / HEAD_DIM
        LN_EPS = 1e-05

        def _layernorm(t, gamma, beta):
            mu = jnp.mean(t, axis=-1, keepdims=True)
            var = jnp.var(t, axis=-1, keepdims=True)
            return (t - mu) * jax.lax.rsqrt(var + LN_EPS) * gamma + beta
        B, N, C = x.shape
        nw = N // WINDOW
        xw = x.reshape(B * nw, WINDOW, C)
        qkv = (xw @ W_qkv).reshape(B * nw, WINDOW, 3, NUM_HEADS, HEAD_DIM)
        q, k, v = (qkv[:, :, 0], qkv[:, :, 1], qkv[:, :, 2])
        q = _layernorm(q, ln_gamma, ln_beta)
        k = _layernorm(k, ln_gamma, ln_beta)
        attn = jnp.einsum('bqhd,bkhd->bhqk', q * SCALE, k)
        attn = jax.nn.softmax(attn, axis=-1)
        out = jnp.einsum('bhqk,bkhd->bqhd', attn, v).reshape(B * nw, WINDOW, C)
        out = out @ W_proj + b_proj
        return out.reshape(B, N, C)

    def _L0_ffn_ref(x, Wqkv, q_scale, k_scale, Wo, ln_g, ln_b, W1, b1, W2, b2):
        import jax, jax.numpy as jnp
        import numpy as np
        DIM = 128
        DEPTH = 6
        HEADS = 16
        DIM_HEAD = 64
        WINDOW = 32
        INNER = HEADS * DIM_HEAD
        DIM_INNER = int(DIM * 4 * 2 / 3)
        QK_SCALE = 8.0

        def shift_tokens(t):
            a, s = jnp.split(t, 2, -1)
            s = jnp.pad(s, ((0, 0), (1, 0), (0, 0)))[:, :-1]
            return jnp.concatenate([a, s], -1)

        def l2norm(t):
            return t / jnp.maximum(jnp.linalg.norm(t, axis=-1, keepdims=True), 1e-12)

        def rotate_half(x):
            x1, x2 = jnp.split(x, 2, -1)
            return jnp.concatenate([-x2, x1], -1)

        def rotary_tables(n):
            half = jnp.arange(0, DIM_HEAD, 2, dtype=jnp.float32)
            inv_freq = 1.0 / 10000.0 ** (half / DIM_HEAD)
            t = jnp.arange(n, dtype=jnp.float32)
            freqs = t[:, None] * inv_freq[None, :]
            freqs = jnp.concatenate([freqs, freqs], -1)
            base_scale = (half + 0.4 * DIM_HEAD) / (1.4 * DIM_HEAD)
            power = (t - n // 2) / (WINDOW // 2)
            scale = base_scale[None, :] ** power[:, None]
            scale = jnp.concatenate([scale, scale], -1)
            return (freqs, scale)

        def local_attention(q, k, v):
            b, h, n, d = q.shape
            w = WINDOW
            nw = n // w
            bq = q.reshape(b, h, nw, w, d)
            bk = k.reshape(b, h, nw, w, d)
            bv = v.reshape(b, h, nw, w, d)

            def look(t):
                p = jnp.pad(t, ((0, 0), (0, 0), (1, 0), (0, 0), (0, 0)))
                return jnp.concatenate([p[:, :, :nw], p[:, :, 1:]], axis=3)
            bk2, bv2 = (look(bk), look(bv))
            seq = jnp.arange(n).reshape(nw, w)
            seq_p = jnp.pad(seq, ((1, 0), (0, 0)), constant_values=-1)
            jt = jnp.concatenate([seq_p[:nw], seq_p[1:]], axis=1)
            it = seq[:, :, None]
            jb = jt[:, None, :]
            mask = (it < jb) | (it > jb + w) | (jb == -1)
            sim = jnp.einsum('bhwie,bhwje->bhwij', bq, bk2) * QK_SCALE
            sim = jnp.where(mask, -jnp.finfo(sim.dtype).max, sim)
            attn = jax.nn.softmax(sim, -1)
            out = jnp.einsum('bhwij,bhwje->bhwie', attn, bv2)
            return out.reshape(b, h, n, d)

        def attn_layer(x, Wqkv, qs, ksc, Wo):
            b, n, _ = x.shape
            qkv = x @ Wqkv
            q, k, v = jnp.split(qkv, 3, -1)
            sh = lambda t: t.reshape(b, n, HEADS, DIM_HEAD).transpose(0, 2, 1, 3)
            q, k, v = (sh(q), sh(k), sh(v))
            q = l2norm(q) * qs
            k = l2norm(k) * ksc
            freqs, scale = rotary_tables(n)
            cos, sin = (jnp.cos(freqs), jnp.sin(freqs))
            q = q * cos * scale + rotate_half(q) * sin * scale
            inv = 1.0 / scale
            k = k * cos * inv + rotate_half(k) * sin * inv
            out = local_attention(q, k, v)
            out = out.transpose(0, 2, 1, 3).reshape(b, n, INNER)
            return out @ Wo

        def ffn_layer(x, g, bln, W1, b1, W2, b2):
            mu = x.mean(-1, keepdims=True)
            var = ((x - mu) ** 2).mean(-1, keepdims=True)
            xn = (x - mu) / jnp.sqrt(var + 1e-05) * g + bln
            hg = xn @ W1 + b1
            a, gate = jnp.split(hg, 2, -1)
            return a * jax.nn.gelu(gate, approximate=False) @ W2 + b2
        for i in range(DEPTH):
            x = attn_layer(shift_tokens(x), Wqkv[i], q_scale[i], k_scale[i], Wo[i]) + x
            x = ffn_layer(shift_tokens(x), ln_g[i], ln_b[i], W1[i], b1[i], W2[i], b2[i]) + x
        return x
    x = L0_attn_x
    x = x + _L0_attn_ref(_layernorm(x, axis=-1), L0_attn_W_qkv, L0_attn_ln_gamma, L0_attn_ln_beta, L0_attn_W_proj, L0_attn_b_proj)
    x = x + _L0_ffn_ref(_layernorm(x, axis=-1), L0_ffn_Wqkv, L0_ffn_q_scale, L0_ffn_k_scale, L0_ffn_Wo, L0_ffn_ln_g, L0_ffn_ln_b, L0_ffn_W1, L0_ffn_b1, L0_ffn_W2, L0_ffn_b2)
    return x

_drawn_inputs = setup_inputs


def setup_inputs(seed=0):
    import zlib

    import numpy as np

    out = dict(_drawn_inputs(seed))
    spreads = {'L0_attn_ln_gamma': (1.0, 0.2),
     'L0_attn_ln_beta': (0.0, 0.1),
     'L0_ffn_q_scale': (1.0, 0.6),
     'L0_ffn_k_scale': (1.0, 0.6),
     'L0_ffn_ln_g': (1.0, 0.6),
     'L0_ffn_ln_b': (0.0, 0.8),
     'L0_ffn_b1': (0.0, 0.8),
     'L0_ffn_b2': (0.0, 0.1)}
    factors = {'L0_attn_b_proj': 3.15, 'L0_ffn_W1': 3.869, 'L0_ffn_W2': 3.804}
    for name, (base, spread) in spreads.items():
        noise = np.random.default_rng([zlib.crc32(name.encode()), seed]).standard_normal(out[name].shape)
        drawn = base * np.exp(spread * noise) if base else spread * noise
        out[name] = jnp.asarray(drawn.astype(out[name].dtype))
    for name, factor in factors.items():
        out[name] = (out[name] * factor).astype(out[name].dtype)
    return out
```

```python
import numpy as np
import concourse.bass as bass
from concourse import mybir
from contextlib import ExitStack

F32 = mybir.dt.float32
F32R = mybir.dt.float32r
I32 = mybir.dt.int32
ALU = mybir.AluOpType
ACT = mybir.ActivationFunctionType
AX = mybir.AxisListType

P = 128
SEQS, LEN, DM = 16, 256, 128
TOKENS = SEQS * LEN
BLOCKS = LEN // P
TILES = TOKENS // P
W1N, H1, DH1 = 64, 16, 8
DEPTH, HEADS, DH, WIN = 6, 16, 64, 32
INNER = HEADS * DH
PAIRS = HEADS // 2
UNIT = 512
UH = UNIT // DH
NQK = 2 * INNER // UNIT
NV = INNER // UNIT
KEYS1 = P + WIN
SW = P + KEYS1
QK_SCALE = 8.0
LN_EPS = 1e-5
HID = int(DM * 4 * 2 / 3)
HTILE = [(0, 128), (128, 128), (256, HID - 256)]
GROUP = 2 * LEN
GROUPS = TOKENS // GROUP
NEG = 3.0e38
LN_IN_SCALE = 65536.0
HALF_LOG = 5.545177444479562


def consts():
    half = np.arange(0, DH, 2, dtype=np.float32)
    inv_freq = (np.float32(1.0) / np.float32(10000.0) ** (half / np.float32(DH))).astype(np.float32)
    t = np.arange(LEN, dtype=np.float32)
    freqs = (t[:, None] * inv_freq[None, :]).astype(np.float32)
    freqs = np.concatenate([freqs, freqs], -1)
    base = (half + np.float32(0.4 * DH)) / np.float32(1.4 * DH)
    power = (t - LEN // 2) / np.float32(WIN // 2)
    scale = (base[None, :].astype(np.float32) ** power[:, None]).astype(np.float32)
    scale = np.concatenate([scale, scale], -1)
    sign = np.concatenate([-np.ones(DH // 2), np.ones(DH // 2)]).astype(np.float32)
    cos, sin = np.cos(freqs), np.sin(freqs)
    rot = np.stack([-QK_SCALE * cos * scale, -QK_SCALE * sin * scale * sign,
                    cos / scale, sin / scale * sign]).astype(np.float32)
    rot = rot.reshape(4, BLOCKS, P, DH).transpose(2, 0, 1, 3).copy()
    i = np.arange(P)[:, None]
    j0, j1 = np.arange(P)[None, :], np.arange(KEYS1)[None, :] - WIN
    mask = np.concatenate([np.where((i < j) | (i > j + WIN), NEG, 0.0) for j in (j0, j1)], 1)
    ident = np.eye(P)
    head_mask = (np.arange(P)[:, None] // DH1 == np.arange(H1)[None, :])
    parity = (np.arange(P)[:, None] // W1N == (np.arange(P)[None, :] // DH1) % 2)
    small = np.concatenate([mask, ident, head_mask, parity], 1).astype(np.float32)
    return rot.reshape(P, -1), small


def build(nc, x_in, w_first, wqkv, wo, qkscale, fw1, fw2, vectors, c_rot, c_small, out):
    ctx = ExitStack()
    with ctx:
        def sb(name, shape, dt=F32):
            return ctx.enter_context(nc.sbuf_tensor(name, shape, dt))

        def sem(name):
            return ctx.enter_context(nc.semaphore(name))

        X1 = sb("X1", [P, TILES, DM])
        xT = sb("xT", [P, TOKENS])
        rot = sb("rot", [P, 4, BLOCKS, DH])
        small = sb("small", [P, SW + P + H1 + P])
        mask = small[:, 0:SW]
        ident = small[:, SW:SW + P]
        head_mask = small[:, SW + P:SW + P + H1]
        parity = small[:, SW + P + H1:]
        wq_raw = sb("wq_raw", [P, 3 * INNER])
        wq_h = sb("wq_h", [P, 3 * INNER], F32R)
        wq_l = sb("wq_l", [P, 3 * INNER], F32R)
        wo_sb = sb("wo_sb", [P, PAIRS, DM])
        w1_raw = sb("w1_raw", [P, 2 * HID])
        w1_h = sb("w1_h", [P, 2 * HID], F32R)
        w1_l = sb("w1_l", [P, 2 * HID], F32R)
        w2_sb = sb("w2_sb", [P, 3, DM])
        vec = sb("vec", [P, 2 + 6 + 1])
        qks = sb("qks", [P, 2, DH])
        tab = sb("tab", [P, 4, BLOCKS, DH])
        xs_h = sb("xs_h", [P, 2, LEN], F32R)
        xs_l = sb("xs_l", [P, 2, LEN], F32R)
        sq = sb("sq", [P, 2, UNIT])
        tc = sb("tc", [P, 2, UNIT])
        ts = sb("ts", [P, 2, UNIT])
        qk = sb("qk", [P, BLOCKS * NQK, UNIT])
        ss = sb("ss", [P, BLOCKS, 2 * HEADS])
        rn0 = sb("rn0", [P, 2 * HEADS])
        rnt = sb("rnt", [P, 2 * HEADS])
        rn = sb("rn", [P, BLOCKS, 2 * HEADS])
        qT = sb("qT", [P, 2, PAIRS, LEN])
        kT = sb("kT", [P, 2, PAIRS, LEN])
        V = sb("V", [P, 2, BLOCKS, INNER])
        NP_ = 4
        SM = sb("SM", [P, 2, SW])
        nmax = sb("nmax", [P, HEADS, 2])
        rsum = sb("rsum", [P, HEADS, 2])
        rden = sb("rden", [P, HEADS, 2])
        ZP = P - WIN
        Pr = sb("Pr", [P, NP_, P + ZP + KEYS1])
        PT = sb("PT", [P, 2, SW])
        oT = sb("oT", [P, PAIRS, LEN])
        banks = [ctx.enter_context(nc.psum_tensor(f"bank{i}", [P, 512], F32)) for i in range(8)]
        QB, TB, SB, PB, OB, YB = banks[0:2], banks[2], banks[3:5], banks[5], banks[6], banks[7]

        COUNTS = {
            "xs_hi": (2, 0),
            "xs_ready": (1, 0),
            "qkv_done": (12, 16),
            "squared": (8, 0),
            "v_kept": (4, 4),
            "rotated": (8, 8),
            "summed": (8, 2),
            "guarded": (2, 0),
            "ln_done": (2, 0),
            "seeded": (2, 0),
            "newton": (4, 0),
            "normed": (2, 2),
            "qk_added": (8, 2),
            "qk_scaled": (8, 8),
            "qkT_done": (8, 8),
            "qkT_kept": (8, 1),
            "s_done": (16, 0),
            "masked": (16, 2),
            "exp_done": (16, 2),
            "recip_done": (16, 0),
            "p_scaled": (16, 0),
            "pT_done": (16, 4),
            "pT_kept": (16, 1),
            "pv_done": (16, 2),
            "oT_kept": (8, 1),
            "y_done": (1, 1),
            "x_updated": (1, 1),
            "f_shifted": (1, 0), "f_t1": (1, 1), "f_stats": (4, 0), "f_chain": (16, 0), "f_normed": (1, 0),
            "f_t2": (1, 0), "f_xn": (1, 0), "f_hi": (1, 0), "f_split": (1, 0), "f_w1": (6, 6),
            "f_gelu": (3, 0), "f_gated": (3, 3), "f_w2": (1, 1), "f_x": (1, 1),
        }
        S = {n: sem(n) for n in (*COUNTS, "phase", "loaded", "attn_loaded", "ffn_loaded", "stored", "step1", "prep", "prep_ffn", "o_copied", "o_t", "o_sum", "zeroed", "waited")}

        class Pass:

            def __init__(self, e, value, offset=0, known=None):
                self.e, self.value, self.offset = e, value, offset
                self.known = {} if known is None else known

            def __add__(self, n):
                return Pass(self.e, self.value, self.offset + n, self.known)

            def times(self, per):
                if per not in self.known:
                    self.known[per] = self.e.snap(self.value * per)
                return self.known[per]

        def wait(e, name, g, k):
            per, ahead = COUNTS[name]
            e.wait_ge(S[name], g.times(per) + (g.offset * per + ahead + k))

        def apart(e):
            e.sem_inc(S["waited"], 1)

        def give_ahead(e):
            for n, (_, ahead) in COUNTS.items():
                if ahead:
                    e.sem_inc(S[n], ahead)
            for n in ("step1", "o_t", "o_sum"):
                e.sem_inc(S[n], 1)
            e.sem_inc(S["phase"], PHASE_AHEAD)

        ENGINES = 4

        MEETINGS = 4
        PHASE_AHEAD = ENGINES + 1

        def meet(e, number):
            e.drain().then_inc(S["phase"], 1)
            e.wait_ge(S["phase"], number * ENGINES + PHASE_AHEAD)
            apart(e)

        block = ctx.enter_context(nc.Block())

        A_xn = tc[:, 0, 0:P]
        A_xnT = tc[:, 0, P:2 * P]
        A_qk = tc[:, 1, 0:2 * P]
        A_qk2 = tc[:, 1, 2 * P:4 * P]
        A_sq = ts[:, 0, 0:2 * P]
        A_w = w1_raw[:, 0:3 * P]
        A_wp = w1_raw[:, 3 * P:4 * P]
        A_bp = w1_raw[:, 4 * P:5 * P]
        A_gb = w1_raw[:, 5 * P:5 * P + 2 * DH1]
        A_st = ss[:, 0, :]
        A_qT = ts[:, 1, 0:P]
        A_twice = ts[:, 1, P:3 * P]
        A_KX = qT[:, :, 0:4, :].rearrange("p a b c -> p a (b c)")
        A_S = kT[:, 0, 0:4, :].rearrange("p b c -> p (b c)")
        A_P = kT[:, 0, 4:8, :].rearrange("p b c -> p (b c)")
        A_PT = kT[:, 1, 0:4, :].rearrange("p b c -> p (b c)")
        A_V = kT[:, 1, 4:5, :].rearrange("p b c -> p (b c)")
        A_o = kT[:, 1, 5, 0:P]
        A_oT = kT[:, 1, 5, P:2 * P]
        A_z = kT[:, 1, 6, 0:P]

        def rsqrt_steps(v, tmp, y):
            return [
                ("act", lambda i: nc.scalar.activation(tmp, v, ACT.Ln, scale=LN_IN_SCALE)),
                ("act", lambda i: nc.scalar.activation(y, tmp, ACT.Exp, scale=-0.5, bias=vec_half[:, 0:1])),
                ("dve", lambda i: nc.vector.scalar_tensor_tensor(tmp, v, -0.5, y, ALU.mult, ALU.mult)),
                ("dve", lambda i: nc.vector.tensor_tensor(tmp, tmp, y, ALU.mult)),
                ("dve", lambda i: nc.vector.scalar_tensor_tensor(y, tmp, 1.5, y, ALU.add, ALU.mult)),
            ]

        vec_half = sb("vec_half", [P, 1])

        def bc(ap, n, inner):
            return ap.rearrange("p (n o) -> p n o", o=1).broadcast_to([P, n, inner])

        def rep(ap, n, inner):
            return ap.rearrange("p (o d) -> p o d", o=1).broadcast_to([P, n, inner])

        def h3(ap, d):
            return ap.rearrange("p (n d) -> p n d", d=d)

        st6, mv, rs1, tmp1 = A_st[:, 0:6], A_st[:, 6:8], A_st[:, 8:9], A_st[:, 9:10]
        mean = rn0[:, :]
        V_ = nc.vector
        T_ = nc.tensor
        A_ = nc.scalar

        stats_steps = []

        def layernorm_steps(src, dst):
            two = (lambda i: V_.bn_stats(st6, src(i)), lambda i: V_.bn_aggr(mv, st6))
            stats_steps.extend(two)
            return [
                ("dve", two[0]),
                ("dve", two[1]),
                ("dve", lambda i: V_.tensor_scalar(mv[:, 1:2], mv[:, 1:2], LN_EPS, None, ALU.add)),
                *rsqrt_steps(mv[:, 1:2], tmp1, rs1),
                ("dve", lambda i: V_.tensor_scalar(dst, src(i), mv[:, 0:1], rs1, ALU.subtract, ALU.mult)),
            ]

        def mm(out, lhsT, rhs, start=True, stop=True, **k):
            return T_.matmul(out, lhsT, rhs, start=start, stop=stop, **k)

        def tr(out, in_, idn=None):
            return T_.transpose(out, in_, ident if idn is None else idn)

        def project_qkv(i):
            mm(QB[0][:, 0:2 * P], A_xnT, A_w[:, 0:2 * P])
            for w in range(2):
                last = mm(QB[1][:, w * P:(w + 1) * P], A_twice[:, w * P:(w + 1) * P], A_w[:, 2 * P:3 * P])
            return last

        def scores1(i):
            for w in range(2):
                for half in range(2):
                    last = mm(SB[half][w * W1N:(w + 1) * W1N, :], A_qT[:, w * W1N:(w + 1) * W1N],
                              A_KX[:, w, half * 512:(half + 1) * 512])
            return last

        def transpose_p(half):
            def f(i):
                for t in range(4):
                    last = tr(banks[half][:, t * P:(t + 1) * P], A_P[:, (4 * half + t) * P:(4 * half + t + 1) * P])
                return last
            return f

        def pv1(i):
            for t in range(8):
                for w in range(2):
                    last = mm(OB[w * W1N:(w + 1) * W1N, t * 16:(t + 1) * 16],
                              A_PT[:, t * P + w * W1N:t * P + (w + 1) * W1N],
                              A_V[:, w * P + t * 16:w * P + (t + 1) * 16])
            return last

        def steps1():
            n32 = 2 * H1
            s = []
            s += layernorm_steps(lambda i: X1[:, i, :], A_xn)
            s.append(("pe", lambda i: tr(TB[:, 0:P], A_xn)))
            s.append(("act", lambda i: A_.activation(A_xnT, TB[:, 0:P], ACT.Copy)))
            s.append(("act", lambda i: A_.activation(
                A_twice.rearrange("p (w r t) -> p w r t", w=2, r=2),
                TB[:, 0:P].rearrange("p (w o t) -> p w o t", w=2, o=1).broadcast_to([P, 2, 2, W1N]), ACT.Copy)))
            s.append(("pe", project_qkv))
            s.append(("dve", lambda i: V_.tensor_tensor(h3(A_V, P), h3(QB[1][:, 0:2 * P], P), rep(parity, 2, P), ALU.mult)))
            s.append(("dve", lambda i: V_.tensor_reduce(mean, h3(QB[0][:, 0:2 * P], DH1), axis=AX.X, op=ALU.add)))
            s.append(("dve", lambda i: V_.tensor_scalar(mean, mean, 1.0 / DH1, None, ALU.mult)))
            s.append(("dve", lambda i: V_.tensor_tensor(h3(A_qk, DH1), h3(QB[0][:, 0:2 * P], DH1), bc(mean, n32, DH1), ALU.subtract)))
            s.append(("dve", lambda i: V_.tensor_tensor(A_sq, A_qk, A_qk, ALU.mult)))
            s.append(("dve", lambda i: V_.tensor_reduce(rnt[:, :], h3(A_sq, DH1), axis=AX.X, op=ALU.add)))
            s.append(("dve", lambda i: V_.tensor_scalar(rnt[:, :], rnt[:, :], 1.0 / DH1, LN_EPS, ALU.mult, ALU.add)))
            s += rsqrt_steps(rnt[:, :], rn0[:, :], rn[:, 0, :])
            s.append(("dve", lambda i: V_.tensor_tensor(h3(A_qk2, DH1), h3(A_qk, DH1), bc(rn[:, 0, :], n32, DH1), ALU.mult)))
            s.append(("dve", lambda i: V_.tensor_tensor(h3(A_qk, DH1), h3(A_qk2, DH1), rep(A_gb[:, 0:DH1], n32, DH1), ALU.mult)))
            s.append(("dve", lambda i: V_.tensor_tensor(h3(A_qk2, DH1), h3(A_qk, DH1), rep(A_gb[:, DH1:2 * DH1], n32, DH1), ALU.add)))
            s.append(("pe", lambda i: (tr(TB[:, 0:P], A_qk2[:, 0:P]), tr(PB[:, 0:P], A_qk2[:, P:2 * P]))[1]))
            s.append(("act", lambda i: A_.activation(A_qT, TB[:, 0:P], ACT.Copy)))
            for w in range(2):
                s.append(("dve", lambda i, w=w: V_.tensor_tensor(
                    h3(A_KX[:, w, :], W1N), rep(PB[:, w * W1N:(w + 1) * W1N], H1, W1N), bc(head_mask, H1, W1N), ALU.mult)))
            s.append(("pe", scores1))
            for half in range(2):
                hh = slice(half * 8, half * 8 + 8)
                s.append(("dve", lambda i, half=half, hh=hh: V_.tensor_reduce(rsum1[:, hh], h3(SB[half][:, :], W1N), axis=AX.X, op=ALU.max)))
            for half in range(2):
                hh = slice(half * 8, half * 8 + 8)
                s.append(("dve", lambda i, half=half, hh=hh: V_.tensor_tensor(
                    h3(A_S[:, half * 512:(half + 1) * 512], W1N), h3(SB[half][:, :], W1N), bc(rsum1[:, hh], 8, W1N), ALU.subtract)))
            s.append(("act", lambda i: A_.activation(A_P, A_S, ACT.Exp)))
            s.append(("dve", lambda i: V_.tensor_reduce(rsum1, h3(A_P, W1N), axis=AX.X, op=ALU.add)))
            s.append(("dve", lambda i: V_.reciprocal(rden1, rsum1)))
            for half in range(2):
                s.append(("pe", transpose_p(half)))
                s.append(("act", lambda i, half=half: A_.activation(A_PT[:, half * 512:(half + 1) * 512], banks[half][:, :], ACT.Copy)))
            s.append(("pe", pv1))
            s.append(("dve", lambda i: V_.tensor_tensor(h3(A_o, DH1), h3(OB[:, 0:P], DH1), bc(rden1, H1, DH1), ALU.mult)))
            s.append(("pe", lambda i: tr(TB[:, 0:P], A_o)))
            s.append(("act", lambda i: A_.activation(A_oT, TB[:, 0:P], ACT.Copy)))
            s.append(("pe", lambda i: mm(YB[:, 0:P], A_oT, A_wp)))
            s.append(("dve", lambda i: V_.tensor_tensor(A_xn, X1[:, i, :], A_bp, ALU.add)))
            s.append(("dve", lambda i: V_.tensor_tensor(X1[:, i, :], YB[:, 0:P], A_xn, ALU.add)))
            s += layernorm_steps(lambda i: X1[:, i, :], A_z)
            s.append(("pe", lambda i: tr(TB[:, 0:P], A_z)))
            s.append(("act", lambda i: A_.activation(xT[:, bass.ds(i * P, P)], TB[:, 0:P], ACT.Copy)))
            return s

        rsum1 = nmax[:, :, :].rearrange("p a b -> p (a b)")[:, 0:H1]
        rden1 = rden[:, :, :].rearrange("p a b -> p (a b)")[:, 0:H1]

        def stage1(e, who):
            steps = steps1()
            n = len(steps)
            with e.Fori(0, TILES) as i:
                for k, (eng, f) in enumerate(steps):
                    if eng == who:
                        e.wait_ge(S["step1"], i * n + (k + 1))
                        if f in stats_steps:
                            apart(e)
                        f(i).then_inc(S["step1"], 1)

        QUNITS = [(b, u) for b in range(BLOCKS) for u in range(NQK)]
        VUNITS = [(b, v) for b in range(BLOCKS) for v in range(NV)]
        NQ = len(QUNITS)
        ORDER = {0: ("q", 0), 1: ("v", 0), 2: ("q", 1), 3: ("v", 1), 4: ("q", 2), 5: ("v", 2), 6: ("q", 3),
                 7: ("v", 3), 8: ("q", 4), 10: ("q", 5), 12: ("q", 6), 14: ("q", 7)}
        UNITS = list(ORDER.values())
        SEED_STEP = {7: 0, 15: 1}
        NEWTON_STEP = {8: 0, 16: 1}
        SCALE_STEP = {8: (0, 1), 9: (2, 3), 16: (4, 5), 17: (6, 7)}
        T_STEP = {10: (0,), 11: (1,), 12: (2,), 13: (3,), 18: (4,), 19: (5, 6), 20: (7,)}
        STEPS = 21
        G_ = nc.gpsimd

        def a_pe(e, n, g, p):
            if n == 0:
                wait(e, "xs_ready", g, 1)
            if n in ORDER:
                kind, i = ORDER[n]
                m = UNITS.index((kind, i))
                back = 0 if m >= 2 else 1
                bkind, bi = UNITS[m - 2]
                if bkind == "q":
                    wait(e, "rotated", g, bi + 1 - back * NQ)
                else:
                    wait(e, "v_kept", g, bi + 1 - back * len(VUNITS))
                b, u = QUNITS[i] if kind == "q" else (VUNITS[i][0], NQK + VUNITS[i][1])
                high, low = (x[:, p, b * P:(b + 1) * P] for x in (xs_h, xs_l))
                cols = slice(u * UNIT, (u + 1) * UNIT)
                bank = QB[m % 2]
                mm(bank[:, :], high, wq_h[:, cols], True, False)
                mm(bank[:, :], low, wq_h[:, cols], False, False)
                mm(bank[:, :], high, wq_l[:, cols], False, True).then_inc(S["qkv_done"], 1)
            for j in T_STEP.get(n, ()):
                wait(e, "qk_scaled", g, j + 1)
                wait(e, "qkT_kept", g, j)
                for t in range(4):
                    last = tr(TB[:, t * P:(t + 1) * P], qk[:, j, t * P:(t + 1) * P])
                last.then_inc(S["qkT_done"], 1)

        def a_act(e, n, g, p):
            if n in ORDER:
                kind, i = ORDER[n]
                m = UNITS.index((kind, i))
                wait(e, "qkv_done", g, m + 1)
                if kind == "q":
                    wait(e, "summed", g, i - 1)
                    A_.activation(sq[:, i % 2, :], QB[m % 2][:, :], ACT.Square).then_inc(S["squared"], 1)
                else:
                    b, v = VUNITS[i]
                    A_.activation(V[:, p, b, v * UNIT:(v + 1) * UNIT], QB[m % 2][:, :],
                                  ACT.Copy).then_inc(S["v_kept"], 1)
            if n in SEED_STEP:
                b = SEED_STEP[n]
                wait(e, "guarded", g, b + 1)
                wait(e, "normed", g, b)
                A_.activation(rnt[:, :], ss[:, b, :], ACT.Ln, scale=LN_IN_SCALE).then_inc(S["ln_done"], 1)
                wait(e, "ln_done", g, b + 1)
                A_.activation(rn0[:, :], rnt[:, :], ACT.Exp, scale=-0.5,
                              bias=vec_half[:, 0:1]).then_inc(S["seeded"], 1)
            for j in T_STEP.get(n, ()):
                b, u = QUNITS[j]
                wait(e, "qkT_done", g, j + 1)
                dst = (qT if u < NQK // 2 else kT)[:, p, (u % 2) * 4:(u % 2) * 4 + 4, b * P:(b + 1) * P]
                A_.activation(dst, TB[:, :].rearrange("p (t c) -> p t c", t=4),
                              ACT.Copy).then_inc(S["qkT_kept"], 1)

        def a_dve(e, n, g, p, at):
            if n == 0:
                wait(e, "xs_hi", g, 2)
                V_.tensor_tensor(xs_l[0:64, p, :], xT[0:64, bass.ds(at, LEN)],
                                 xs_h[0:64, p, :].bitcast(F32), ALU.subtract)
                V_.tensor_tensor(xs_l[64:P, p, 1:LEN], xT[64:P, bass.ds(at, LEN - 1)],
                                 xs_h[64:P, p, 1:LEN].bitcast(F32), ALU.subtract).then_inc(S["xs_ready"], 1)
            if n in ORDER and ORDER[n][0] == "q":
                i = ORDER[n][1]
                m = UNITS.index(ORDER[n])
                b, u = QUNITS[i]
                kind = 0 if u < NQK // 2 else 2
                bank = QB[m % 2]
                wait(e, "squared", g, i + 1)
                wait(e, "qk_added", g, i - 1)
                V_.tensor_tensor(h3(tc[:, i % 2, :], DH), h3(bank[:, :], DH), rep(tab[:, kind, b, :], UH, DH), ALU.mult)
                halves = dict(a=2, c=DH // 2)
                swapped = bank[:, :].rearrange("p (h a c) -> p h a c", **halves)[:, :, ::-1, :]
                sines = tab[:, kind + 1, b, :].rearrange("p (o a c) -> p o a c", o=1, a=2).broadcast_to([P, UH, 2, DH // 2])
                V_.tensor_tensor(ts[:, i % 2, :].rearrange("p (h a c) -> p h a c", **halves),
                                 swapped, sines, ALU.mult).then_inc(S["rotated"], 1)
                V_.tensor_reduce(ss[:, b, u * UH:(u + 1) * UH], h3(sq[:, i % 2, :], DH), axis=AX.X,
                                 op=ALU.add).then_inc(S["summed"], 1)
                if u == NQK - 1:
                    wait(e, "summed", g, i + 1)
                    V_.tensor_scalar(ss[:, b, :], ss[:, b, :], 1e-24, None, ALU.max).then_inc(S["guarded"], 1)
            if n in NEWTON_STEP:
                b = NEWTON_STEP[n]
                wait(e, "seeded", g, b + 1)
                V_.scalar_tensor_tensor(rnt[:, :], ss[:, b, :], -0.5, rn0[:, :], ALU.mult,
                                        ALU.mult).then_inc(S["newton"], 1)
                wait(e, "newton", g, 2 * b + 1)
                V_.tensor_tensor(rnt[:, :], rnt[:, :], rn0[:, :], ALU.mult).then_inc(S["newton"], 1)
                wait(e, "newton", g, 2 * b + 2)
                wait(e, "qk_scaled", g, 4 * b + 4 - NQ)
                V_.scalar_tensor_tensor(rn[:, b, :], rnt[:, :], 1.5, rn0[:, :], ALU.add,
                                        ALU.mult).then_inc(S["normed"], 1)

        def a_pool(e, n, g):
            if n in ORDER and ORDER[n][0] == "q":
                i = ORDER[n][1]
                wait(e, "rotated", g, i + 1)
                wait(e, "qkT_done", g, i + 1 - NQ)
                G_.tensor_tensor(qk[:, i, :], tc[:, i % 2, :], ts[:, i % 2, :], ALU.add).then_inc(S["qk_added"], 1)
            for j in SCALE_STEP.get(n, ()):
                b, u = QUNITS[j]
                wait(e, "normed", g, b + 1)
                wait(e, "qk_added", g, j + 1)
                G_.tensor_tensor(h3(qk[:, j, :], DH), h3(qk[:, j, :], DH),
                                 bc(rn[:, b, u * UH:(u + 1) * UH], UH, DH), ALU.mult).then_inc(S["qk_scaled"], 1)

        def b_pe(e, n, g, p):
            if n < HEADS:
                r = (n % 2) * DH
                if n == 0:
                    wait(e, "qkT_kept", g, NQ)
                    wait(e, "v_kept", g, len(VUNITS))
                wait(e, "masked", g, n - 1)
                q, k = qT[r:r + DH, p, n // 2, :], kT[r:r + DH, p, n // 2, :]
                mm(SB[n % 2][:, 0:P], q[:, 0:P], k[:, 0:P])
                mm(SB[n % 2][:, P:SW], q[:, P:LEN], k[:, P - WIN:LEN]).then_inc(S["s_done"], 1)

        def b_pe_late(e, n, g, p):
            h = n - 2
            if 0 <= h < HEADS:
                wait(e, "p_scaled", g, h + 1)
                wait(e, "pT_kept", g, h)
                pr = Pr[:, h % NP_, :]
                tr(PB[:, 0:P], pr[:, 0:P])
                tr(PB[:, P:KEYS1], pr[0:WIN, P:2 * P], ident[0:WIN, 0:WIN])
                tr(PB[:, KEYS1:SW], pr[:, 2 * P:3 * P]).then_inc(S["pT_done"], 1)
            h = n - 3
            if 0 <= h < HEADS:
                r = (h % 2) * DH
                wait(e, "pT_kept", g, h + 1)
                if h % 2 == 0:
                    wait(e, "oT_kept", g, h // 2)
                v = [V[:, p, b, h * DH:(h + 1) * DH] for b in range(BLOCKS)]
                mm(OB[r:r + DH, 0:KEYS1], v[0], PT[:, h % 2, 0:KEYS1], True, False, skip_group_check=True)
                mm(OB[r:r + DH, P:LEN], v[1], PT[:, h % 2, KEYS1:SW], False, True,
                   skip_group_check=True).then_inc(S["pv_done"], 1)
            j = (n - 6) // 2
            if n % 2 == 0 and 0 <= j < PAIRS:
                wait(e, "oT_kept", g, j + 1)
                if j == 0:
                    wait(e, "x_updated", g, 0)
                last = mm(YB[:, 0:LEN], wo_sb[:, j, :], oT[:, j, :], j == 0, j == PAIRS - 1)
                if j == PAIRS - 1:
                    last.then_inc(S["y_done"], 1)

        def b_dve(e, n, g):
            if n < HEADS:
                wait(e, "s_done", g, n + 1)
                wait(e, "exp_done", g, n - 1)
                apart(e)
                for b, (lo, hi) in enumerate(((0, P), (P, SW))):
                    last = V_.tensor_tensor_reduce(
                        out=SM[:, n % 2, lo:hi], in0=SB[n % 2][:, lo:hi], in1=mask[:, lo:hi], scale=1.0,
                        scalar=NEG, op0=ALU.add, op1=ALU.min, accum_out=nmax[:, n, b:b + 1])
                last.then_inc(S["masked"], 1)

        def b_dve_late(e, n, g):
            h = n - 1
            if 0 <= h < HEADS:
                wait(e, "exp_done", g, h + 1)
                V_.reciprocal(rden[:, h, :], rsum[:, h, :]).then_inc(S["recip_done"], 1)
            h = n - 2
            if 0 <= h < HEADS:
                wait(e, "pT_done", g, h + 1)
                wait(e, "pv_done", g, h - 1)
                V_.tensor_copy(PT[:, h % 2, :], PB[:, 0:SW]).then_inc(S["pT_kept"], 1)

        def b_act(e, n, g):
            h = n - 1
            if 0 <= h < HEADS:
                wait(e, "masked", g, h + 1)
                wait(e, "pT_done", g, h + 1 - NP_)
                pr = Pr[:, h % NP_, :]
                A_.activation(pr[:, 0:P], SM[:, h % 2, 0:P], ACT.Exp, scale=-1.0, bias=nmax[:, h, 0:1],
                              accum_out=rsum[:, h, 0:1])
                A_.activation(pr[:, P + ZP:], SM[:, h % 2, P:SW], ACT.Exp, scale=-1.0, bias=nmax[:, h, 1:2],
                              accum_out=rsum[:, h, 1:2]).then_inc(S["exp_done"], 1)

        def b_act_late(e, n, g):
            j = (n - 4) // 2
            if n % 2 == 0 and 0 <= j < PAIRS:
                wait(e, "pv_done", g, 2 * j + 2)
                if j == 0:
                    wait(e, "y_done", g, 0)
                A_.activation(oT[:, j, :], OB[:, 0:LEN], ACT.Copy).then_inc(S["oT_kept"], 1)

        def b_pool(e, n, g):
            h = n - 1
            if 0 <= h < HEADS:
                wait(e, "recip_done", g, h + 1)
                pr = Pr[:, h % NP_, :]
                G_.tensor_tensor(pr[:, 0:P], pr[:, 0:P], rden[:, h, 0:1].broadcast_to([P, P]), ALU.mult)
                G_.tensor_tensor(pr[:, P + ZP:], pr[:, P + ZP:], rden[:, h, 1:2].broadcast_to([P, KEYS1]),
                                 ALU.mult).then_inc(S["p_scaled"], 1)

        def pass_pe(e, g, p, at, b, a):
            for n in range(STEPS):
                if b:
                    b_pe(e, n, g, p)
                if a:
                    a_pe(e, n, g + 1, 1 - p)
                if b:
                    b_pe_late(e, n, g, p)

        def pass_act(e, g, p, at, b, a):
            if a:
                wait(e, "qkv_done", g + 1, -12)
                A_.activation(xs_h[0:64, 1 - p, :], xT[0:64, bass.ds(at + LEN, LEN)], ACT.Copy).then_inc(S["xs_hi"], 1)
                A_.activation(xs_h[64:P, 1 - p, 1:LEN], xT[64:P, bass.ds(at + LEN, LEN - 1)],
                              ACT.Copy).then_inc(S["xs_hi"], 1)
            for n in range(STEPS):
                if b:
                    b_act(e, n, g)
                if a:
                    a_act(e, n, g + 1, 1 - p)
                if b:
                    b_act_late(e, n, g)

        def pass_dve(e, g, p, at, b, a):
            for n in range(STEPS):
                if b:
                    b_dve(e, n, g)
                if a:
                    a_dve(e, n, g + 1, 1 - p, at + LEN)
                if b:
                    b_dve_late(e, n, g)
            if b:
                wait(e, "y_done", g, 1)
                V_.tensor_tensor(xT[:, bass.ds(at, LEN)], YB[:, 0:LEN], xT[:, bass.ds(at, LEN)],
                                 ALU.add).then_inc(S["x_updated"], 1)

        def pass_pool(e, g, p, at, b, a):
            for n in range(STEPS):
                if b:
                    b_pool(e, n, g)
                if a:
                    a_pool(e, n, g + 1)

        def attention(e, layer, one_pass):
            first = Pass(e, e.snap(layer * SEQS))
            one_pass(e, first + -1, 1, -LEN, False, True)
            with e.Fori(0, SEQS // 2 - 1) as i:
                g = Pass(e, e.snap(layer * SEQS + i * 2))
                at = e.snap(i * (2 * LEN))
                one_pass(e, g, 0, at, True, True)
                one_pass(e, g + 1, 1, at + LEN, True, True)
            one_pass(e, first + (SEQS - 2), 0, (SEQS - 2) * LEN, True, True)
            one_pass(e, first + (SEQS - 1), 1, (SEQS - 1) * LEN, True, False)

        FT1, FT2, FW, FY = banks[0], banks[1], banks[2:6], banks[6]
        xf = qk[:, 0, :]
        xn = h3(qk[:, 1, :], P)
        xnf = qk[:, 2, :]
        f_h, f_l = (x[:, :, :].rearrange("p a b -> p (a b)") for x in (xs_h, xs_l))
        gate = qk[:, 3:6, :]
        hid = [sq[:, 0, :], sq[:, 1, :], tc[:, 0, :]]
        f_st = ts[:, 0, 0:24]
        f_mv = ts[:, 0, 32:40].rearrange("p (t c) -> p t c", c=2)
        f_v, f_y, f_t, f_i = (ts[:, 0, 48 + 8 * k:48 + 8 * k + 4] for k in range(4))
        NT = GROUP // P
        F_ORDER = [(j, k) for j in range(3) for k in (1, 0)]

        def f_pe_w1(e, g):
            wait(e, "f_split", g, 1)
            for m, (j, k) in enumerate(F_ORDER):
                lo, size = HTILE[j]
                if m < 4:
                    wait(e, "f_gated", g, 0)
                elif k:
                    wait(e, "f_gelu", g, j - 1)
                else:
                    wait(e, "f_gated", g, j - 1)
                c = slice(k * HID + lo, k * HID + lo + size)
                bank = FW[m % 4]
                mm(bank[0:size, :], w1_h[:, c], f_h, True, False)
                mm(bank[0:size, :], w1_l[:, c], f_h, False, False)
                mm(bank[0:size, :], w1_h[:, c], f_l, False, True).then_inc(S["f_w1"], 1)

        def f_pe_t1(e, g):
            wait(e, "f_shifted", g, 1)
            for t in range(NT):
                last = tr(FT1[:, t * P:(t + 1) * P], xf[:, t * P:(t + 1) * P])
            last.then_inc(S["f_t1"], 1)

        def f_pe_w2(e, g):
            wait(e, "f_x", g, 0)
            for j, (lo, size) in enumerate(HTILE):
                wait(e, "f_gated", g, j + 1)
                last = mm(FY[:, :], w2_sb[0:size, j, :], hid[j][0:size, :], j == 0, j == 2)
            last.then_inc(S["f_w2"], 1)

        def f_pe_t2(e, g):
            wait(e, "f_normed", g, 1)
            for t in range(NT):
                last = tr(FT2[:, t * P:(t + 1) * P], xn[:, t, :])
            last.then_inc(S["f_t2"], 1)

        def f_act_gelu(e, g):
            for j, (lo, size) in enumerate(HTILE):
                wait(e, "f_w1", g, 2 * j + 1)
                wait(e, "f_gated", g, j - 2)
                A_.activation(gate[0:size, j, :], FW[(2 * j) % 4][0:size, :], ACT.Gelu,
                              bias=vec[0:size, 5 + j:6 + j]).then_inc(S["f_gelu"], 1)

        def f_act_scale(e, g):
            wait(e, "f_t2", g, 1)
            A_.activation(xnf, FT2[:, :], ACT.Identity, scale=vec[:, 0:1], bias=vec[:, 1:2]).then_inc(S["f_xn"], 1)
            wait(e, "f_w1", g, 0)
            wait(e, "f_xn", g, 1)
            A_.activation(f_h, xnf, ACT.Copy).then_inc(S["f_hi"], 1)

        def f_dve_shift(e, g, at):
            wait(e, "f_t1", g, 0)
            V_.tensor_copy(xf[0:64, :], xT[0:64, bass.ds(at, GROUP)])
            two = dict(a=2, c=LEN)
            V_.tensor_copy(xf[64:P, :].rearrange("p (a c) -> p a c", **two)[:, :, 1:],
                           xT[64:P, bass.ds(at, GROUP)].rearrange("p (a c) -> p a c", **two)[:, :, 0:LEN - 1]
                           ).then_inc(S["f_shifted"], 1)

        def f_dve_norm(e, g):
            wait(e, "f_t1", g, 1)
            apart(e)
            for t in range(NT):
                last = V_.bn_stats(f_st[:, 6 * t:6 * t + 6], FT1[:, t * P:(t + 1) * P])
                last.then_inc(S["f_stats"], 1)
            wait(e, "f_stats", g, NT)
            apart(e)
            n = 0

            def chain(ins):
                nonlocal n
                n += 1
                ins.then_inc(S["f_chain"], 1)
                wait(e, "f_chain", g, n)
                if n < NT:
                    apart(e)

            for t in range(NT):
                chain(V_.bn_aggr(f_mv[:, t, :], f_st[:, 6 * t:6 * t + 6]))
            chain(V_.tensor_scalar(f_v, f_mv[:, :, 1], LN_EPS, None, ALU.add))
            chain(V_.tensor_scalar(f_i.bitcast(I32), f_v.bitcast(I32), 1, None, ALU.logical_shift_right))
            chain(V_.tensor_scalar(f_y.bitcast(I32), f_i.bitcast(I32), -1.0, 1597463007.0, ALU.mult, ALU.add))
            for _ in range(3):
                chain(V_.scalar_tensor_tensor(f_t, f_v, -0.5, f_y, ALU.mult, ALU.mult))
                chain(V_.tensor_tensor(f_t, f_t, f_y, ALU.mult))
                chain(V_.scalar_tensor_tensor(f_y, f_t, 1.5, f_y, ALU.add, ALU.mult))
            for t in range(NT):
                last = V_.tensor_scalar(xn[:, t, :], FT1[:, t * P:(t + 1) * P], f_mv[:, t, 0:1], f_y[:, t:t + 1],
                                        ALU.subtract, ALU.mult)
            last.then_inc(S["f_normed"], 1)
            assert n == COUNTS["f_chain"][0], n

        def f_dve_gate(e, g):
            for j, (lo, size) in enumerate(HTILE):
                wait(e, "f_w1", g, 2 * j + 2)
                wait(e, "f_gelu", g, j + 1)
                if j == 0:
                    wait(e, "f_w2", g, 0)
                V_.scalar_tensor_tensor(hid[j][0:size, :], FW[(2 * j + 1) % 4][0:size, :], vec[0:size, 2 + j:3 + j],
                                        gate[0:size, j, :], ALU.add, ALU.mult).then_inc(S["f_gated"], 1)

        def f_dve_split(e, g):
            wait(e, "f_hi", g, 1)
            V_.tensor_tensor(f_l, xnf, f_h.bitcast(F32), ALU.subtract).then_inc(S["f_split"], 1)

        def f_dve_x(e, g, at):
            wait(e, "f_w2", g, 1)
            V_.scalar_tensor_tensor(xT[:, bass.ds(at, GROUP)], FY[:, :], vec[:, 8:9], xT[:, bass.ds(at, GROUP)],
                                    ALU.add, ALU.add).then_inc(S["f_x"], 1)

        def ffn_pe(e, g, at, b, a):
            if b:
                f_pe_w1(e, g)
            if a:
                f_pe_t1(e, g + 1)
            if b:
                f_pe_w2(e, g)
            if a:
                f_pe_t2(e, g + 1)

        def ffn_act(e, g, at, b, a):
            if b:
                f_act_gelu(e, g)
            if a:
                f_act_scale(e, g + 1)

        def ffn_dve(e, g, at, b, a):
            if a:
                f_dve_shift(e, g + 1, at + GROUP)
            if b:
                f_dve_gate(e, g)
            if a:
                f_dve_norm(e, g + 1)
            if b:
                f_dve_x(e, g, at)
            if a:
                f_dve_split(e, g + 1)

        def feed_forward(e, layer, one_pass):
            first = Pass(e, e.snap(layer * GROUPS))
            one_pass(e, first + -1, -GROUP, False, True)
            with e.Fori(0, GROUPS - 1) as i:
                at = e.snap(i * GROUP)
                one_pass(e, Pass(e, e.snap(layer * GROUPS + i)), at, True, True)
            one_pass(e, first + (GROUPS - 1), (GROUPS - 1) * GROUP, True, False)

        C3 = 3 * INNER
        CA = C3 // 2

        def prepare_act(e, layer):
            e.wait_ge(S["attn_loaded"], layer * 48 + 48)
            A_.activation(wq_h[:, 0:CA], wq_raw[:, 0:CA], ACT.Copy).then_inc(S["prep"], 1)
            A_.activation(wq_h[:, CA:], wq_raw[:, CA:], ACT.Copy).then_inc(S["prep"], 1)

        def prepare_dve(e, layer):
            for x in (xs_h, xs_l):
                V_.memset(x[64:P, :, 0:1].bitcast(F32), 0.0)
            e.wait_ge(S["attn_loaded"], layer * 48 + 48)
            swapped = [qks[:, i, :].rearrange("p (o a c) -> p o a c", o=1, a=2)[:, :, ::-1, :]
                       .broadcast_to([P, BLOCKS, 2, DH // 2]) for i in range(2)]
            for i in range(2):
                V_.tensor_tensor(tab[:, 2 * i, :, :], rot[:, 2 * i, :, :], rep(qks[:, i, :], BLOCKS, DH), ALU.mult)
                V_.tensor_tensor(tab[:, 2 * i + 1, :, :].rearrange("p b (a c) -> p b a c", a=2),
                                 rot[:, 2 * i + 1, :, :].rearrange("p b (a c) -> p b a c", a=2), swapped[i], ALU.mult)
            e.wait_ge(S["prep"], layer * 2 + 1)
            V_.tensor_tensor(wq_l[:, 0:CA], wq_raw[:, 0:CA], wq_h[:, 0:CA].bitcast(F32), ALU.subtract)

        def prepare_pool(e, layer):
            e.wait_ge(S["prep"], layer * 2 + 2)
            G_.tensor_tensor(wq_l[:, CA:], wq_raw[:, CA:], wq_h[:, CA:].bitcast(F32), ALU.subtract)

        def prepare_ffn_act(e, layer):
            e.wait_ge(S["ffn_loaded"], layer * 48 + 48)
            A_.activation(w1_h[:, :], w1_raw[:, :], ACT.Copy).then_inc(S["prep_ffn"], 1)

        def prepare_ffn_dve(e, layer):
            e.wait_ge(S["ffn_loaded"], layer * 48 + 48)
            V_.memset(xf[64:P, :].rearrange("p (a c) -> p a c", a=2)[:, :, 0:1], 0.0)
            e.wait_ge(S["prep_ffn"], layer + 1)
            V_.tensor_tensor(w1_l[:, :], w1_raw[:, :], w1_h[:, :].bitcast(F32), ALU.subtract)

        o_in = qk[:, 0, :]
        o_out = qk[:, 1:3, :]

        def finish(e, who):
            with e.Fori(0, GROUPS) as i:
                if who == "act":
                    e.wait_ge(S["o_t"], i + 1)
                    A_.activation(o_in, xT[:, bass.ds(i * GROUP, GROUP)], ACT.Copy).then_inc(S["o_copied"], 1)
                if who == "pe":
                    e.wait_ge(S["o_copied"], i + 1)
                    e.wait_ge(S["o_sum"], i + 1)
                    for t in range(NT):
                        last = tr(FT1[:, t * P:(t + 1) * P], o_in[:, t * P:(t + 1) * P])
                    last.then_inc(S["o_t"], 1)
                if who == "dve":
                    e.wait_ge(S["o_t"], i + 2)
                    V_.tensor_tensor(X1[:, bass.ds(i * NT, NT), :], X1[:, bass.ds(i * NT, NT), :],
                                     h3(FT1[:, :], P), ALU.add).then_inc(S["o_sum"], 1)

        def program(e, who, one_pass, prepare, one_ffn, prepare_ffn):
            stage1(e, who)
            meet(e, 1)
            with e.Fori(0, DEPTH) as layer:
                if prepare:
                    prepare(e, layer)
                meet(e, layer * MEETINGS + 2)
                attention(e, layer, one_pass)
                meet(e, layer * MEETINGS + 3)
                if prepare_ffn:
                    prepare_ffn(e, layer)
                meet(e, layer * MEETINGS + 4)
                if one_ffn:
                    feed_forward(e, layer, one_ffn)
                meet(e, layer * MEETINGS + 5)
            finish(e, who)

        @block.sync
        def _(sp):
            for dst, src in ((X1[:, :, :], x_in.rearrange("(t p) d -> p t d", p=P)), (small[:, :], c_small),
                             (w1_raw[:, 0:w_first.shape[1]], w_first),
                             (rot[:, :, :, :].rearrange("p a b c -> p (a b c)"), c_rot)):
                sp.dma_start(dst, src).then_inc(S["loaded"], 16)
            with sp.Fori(0, DEPTH) as layer:
                sp.wait_ge(S["phase"], layer * (MEETINGS * ENGINES) + 1)
                sp.dma_start(wq_raw[:, :], wqkv[layer, :, :]).then_inc(S["attn_loaded"], 16)
                sp.dma_start(wo_sb[:, :, :].rearrange("p a b -> p (a b)"), wo[layer, :, :]).then_inc(S["attn_loaded"], 16)
                sp.dma_start(qks[:, :, :].rearrange("p a b -> p (a b)"), qkscale[layer, :, :]).then_inc(S["attn_loaded"], 16)
                sp.wait_ge(S["phase"], layer * (MEETINGS * ENGINES) + ENGINES + PHASE_AHEAD)
                sp.dma_start(w1_raw[:, :], fw1[layer, :, :]).then_inc(S["ffn_loaded"], 16)
                sp.dma_start(w2_sb[:, :, :].rearrange("p a b -> p (a b)"), fw2[layer, :, :]).then_inc(S["ffn_loaded"], 16)
                sp.dma_start(vec[:, :], vectors[layer, :, :]).then_inc(S["ffn_loaded"], 16)
            o = out.rearrange("(t p) d -> p t d", p=P)
            for i in range(GROUPS):
                sp.wait_ge(S["o_sum"], i + 2)
                sp.dma_start(o[:, i * NT:(i + 1) * NT, :], X1[:, i * NT:(i + 1) * NT, :]).then_inc(S["stored"], 16)
            sp.wait_ge(S["stored"], 16 * GROUPS)

        @block.gpsimd
        def _(pool):
            give_ahead(pool)
            G_.memset(Pr[:, :, :], 0.0).then_inc(S["zeroed"], 1)
            G_.memset(vec_half[:, :], HALF_LOG).then_inc(S["zeroed"], 1)
            program(pool, "pool", pass_pool, prepare_pool, None, None)

        @block.scalar
        def _(act):
            act.wait_ge(S["loaded"], 64)
            act.wait_ge(S["zeroed"], 2)
            program(act, "act", pass_act, prepare_act, ffn_act, prepare_ffn_act)

        @block.vector
        def _(dve):
            dve.wait_ge(S["loaded"], 64)
            program(dve, "dve", pass_dve, prepare_dve, ffn_dve, prepare_ffn_dve)

        @block.tensor
        def _(pe):
            pe.wait_ge(S["loaded"], 64)
            program(pe, "pe", pass_pe, None, ffn_pe, None)


def kernel(L0_attn_x, L0_attn_W_qkv, L0_attn_ln_gamma, L0_attn_ln_beta, L0_attn_W_proj, L0_attn_b_proj, L0_ffn_Wqkv,
           L0_ffn_q_scale, L0_ffn_k_scale, L0_ffn_Wo, L0_ffn_ln_g, L0_ffn_ln_b, L0_ffn_W1, L0_ffn_b1, L0_ffn_W2,
           L0_ffn_b2):
    import concourse.bacc as bacc
    from concourse.bass_utils import run_bass_kernel_spmd

    a = lambda x: np.ascontiguousarray(x)
    wide = lambda x: np.broadcast_to(a(x)[None, :], (P, x.shape[0]))
    first = np.concatenate([a(L0_attn_W_qkv), a(L0_attn_W_proj), wide(L0_attn_b_proj), wide(L0_attn_ln_gamma),
                            wide(L0_attn_ln_beta)], 1)
    scales = np.stack([a(L0_ffn_q_scale), a(L0_ffn_k_scale)], 1).reshape(DEPTH, 1, 2 * DH)
    w2 = np.zeros((DEPTH, 3 * P, DM), np.float32)
    w2[:, :HID] = a(L0_ffn_W2)
    vectors = np.zeros((DEPTH, P, 9), np.float32)
    vectors[:, :, 0], vectors[:, :, 1], vectors[:, :, 8] = a(L0_ffn_ln_g), a(L0_ffn_ln_b), a(L0_ffn_b2)
    for k in range(2):
        for j, (lo, size) in enumerate(HTILE):
            vectors[:, :size, 2 + 3 * k + j] = a(L0_ffn_b1)[:, k * HID + lo:k * HID + lo + size]
    c_rot, c_small = consts()
    arrays = {
        "x_in": a(L0_attn_x).reshape(TOKENS, DM),
        "w_first": first,
        "wqkv": a(L0_ffn_Wqkv),
        "wo": a(L0_ffn_Wo).reshape(DEPTH, PAIRS, P, DM).transpose(0, 2, 1, 3).reshape(DEPTH, P, PAIRS * DM),
        "qkscale": np.broadcast_to(scales, (DEPTH, P, 2 * DH)),
        "fw1": a(L0_ffn_W1),
        "fw2": w2.reshape(DEPTH, 3, P, DM).transpose(0, 2, 1, 3).reshape(DEPTH, P, 3 * DM),
        "vectors": vectors,
        "c_rot": c_rot,
        "c_small": c_small,
    }
    arrays = {k: np.ascontiguousarray(v) for k, v in arrays.items()}
    nc = bacc.Bacc("TRN2", target_bir_lowering=False, num_devices=1)
    args = [nc.dram_tensor(k, v.shape, mybir.dt.from_np(v.dtype), kind="ExternalInput").ap() for k, v in arrays.items()]
    out = nc.dram_tensor("out", (TOKENS, DM), F32, kind="ExternalOutput").ap()
    build(nc, *args, out)
    r = run_bass_kernel_spmd(nc, [arrays], core_ids=[0])
    return r.results[0]["out"].reshape(SEQS, LEN, DM)
```

```python
import numpy as np
import concourse.bass as bass
from concourse import mybir
from contextlib import ExitStack

F32 = mybir.dt.float32
F32R = mybir.dt.float32r
I32 = mybir.dt.int32
ALU = mybir.AluOpType
ACT = mybir.ActivationFunctionType
AX = mybir.AxisListType

P = 128
SEQS, LEN, DM = 16, 256, 128
TOKENS = SEQS * LEN
BLOCKS = LEN // P
TILES = TOKENS // P
W1N, H1, DH1 = 64, 16, 8
DEPTH, HEADS, DH, WIN = 6, 16, 64, 32
INNER = HEADS * DH
PAIRS = HEADS // 2
OH = 4
OBATCHES = HEADS // OH
UNIT = 512
UH = UNIT // DH
NQK = 2 * INNER // UNIT
NV = INNER // UNIT
KEYS1 = P + WIN
SW = P + KEYS1
QK_SCALE = 8.0
LN_EPS = 1e-5
HID = int(DM * 4 * 2 / 3)
HTILE = [(0, 128), (128, 128), (256, HID - 256)]
GROUP = 2 * LEN
GROUPS = TOKENS // GROUP
NEG = 3.0e38
LN_IN_SCALE = 65536.0
HALF_LOG = 5.545177444479562


def consts():
    half = np.arange(0, DH, 2, dtype=np.float32)
    inv_freq = (np.float32(1.0) / np.float32(10000.0) ** (half / np.float32(DH))).astype(np.float32)
    t = np.arange(LEN, dtype=np.float32)
    freqs = (t[:, None] * inv_freq[None, :]).astype(np.float32)
    freqs = np.concatenate([freqs, freqs], -1)
    base = (half + np.float32(0.4 * DH)) / np.float32(1.4 * DH)
    power = (t - LEN // 2) / np.float32(WIN // 2)
    scale = (base[None, :].astype(np.float32) ** power[:, None]).astype(np.float32)
    scale = np.concatenate([scale, scale], -1)
    sign = np.concatenate([-np.ones(DH // 2), np.ones(DH // 2)]).astype(np.float32)
    cos, sin = np.cos(freqs), np.sin(freqs)
    rot = np.stack([-QK_SCALE * cos * scale, -QK_SCALE * sin * scale * sign,
                    cos / scale, sin / scale * sign]).astype(np.float32)
    rot = rot.reshape(4, BLOCKS, P, DH).transpose(2, 0, 1, 3).copy()
    i = np.arange(P)[:, None]
    j0, j1 = np.arange(P)[None, :], np.arange(KEYS1)[None, :] - WIN
    mask = np.concatenate([np.where((i < j) | (i > j + WIN), NEG, 0.0) for j in (j0, j1)], 1)
    ident = np.eye(P)
    head_mask = (np.arange(P)[:, None] // DH1 == np.arange(H1)[None, :])
    parity = (np.arange(P)[:, None] // W1N == (np.arange(P)[None, :] // DH1) % 2)
    small = np.concatenate([mask, ident, head_mask, parity], 1).astype(np.float32)
    return rot.reshape(P, -1), small


def build(nc, x_in, w_first, wqkv, wo, qkscale, fw1, fw2, vectors, c_rot, c_small, out):
    ctx = ExitStack()
    with ctx:
        def sb(name, shape, dt=F32):
            return ctx.enter_context(nc.sbuf_tensor(name, shape, dt))

        def sem(name):
            return ctx.enter_context(nc.semaphore(name))

        X1 = sb("X1", [P, TILES, DM])
        xT = sb("xT", [P, TOKENS])
        rot = sb("rot", [P, 4, BLOCKS, DH])
        small = sb("small", [P, SW + P + H1 + P])
        mask = small[:, 0:SW]
        ident = small[:, SW:SW + P]
        head_mask = small[:, SW + P:SW + P + H1]
        parity = small[:, SW + P + H1:]
        wq_raw = sb("wq_raw", [P, 3 * INNER])
        wq_h = sb("wq_h", [P, 3 * INNER], F32R)
        wq_l = sb("wq_l", [P, 3 * INNER], F32R)
        wo_sb = sb("wo_sb", [P, PAIRS, DM])
        w1_raw = sb("w1_raw", [P, 2 * HID])
        w1_h = sb("w1_h", [P, 2 * HID], F32R)
        w1_l = sb("w1_l", [P, 2 * HID], F32R)
        w2_sb = sb("w2_sb", [P, 3, DM])
        vec = sb("vec", [P, 2 + 6 + 1])
        qks = sb("qks", [P, 2, DH])
        tab = sb("tab", [P, 4, BLOCKS, DH])
        xs_h = sb("xs_h", [P, 2, LEN], F32R)
        xs_l = sb("xs_l", [P, 2, LEN], F32R)
        sq = sb("sq", [P, 2, UNIT])
        tc = sb("tc", [P, 2, UNIT])
        ts = sb("ts", [P, 2, UNIT])
        qk = sb("qk", [P, BLOCKS * NQK, UNIT])
        ss = sb("ss", [P, BLOCKS, 2 * HEADS])
        rn0 = sb("rn0", [P, 2 * HEADS])
        rnt = sb("rnt", [P, 2 * HEADS])
        rn = sb("rn", [P, BLOCKS, 2 * HEADS])
        qT = sb("qT", [P, 2, PAIRS, LEN])
        kT = sb("kT", [P, 2, PAIRS, LEN])
        V = sb("V", [P, 2, BLOCKS, INNER])
        NP_ = 4
        SM = sb("SM", [P, 2, SW])
        nmax = sb("nmax", [P, HEADS, 2])
        rsum = sb("rsum", [P, BLOCKS, HEADS])
        rden = sb("rden", [P, BLOCKS, HEADS])
        ZP = P - WIN
        Pr = sb("Pr", [P, NP_, P + ZP + KEYS1])
        NT_ = 3
        PT = sb("PT", [P, NT_, SW])
        osb = sb("osb", [P, BLOCKS, OH * DH])
        oT = sb("oT", [P, PAIRS, LEN])
        banks = [ctx.enter_context(nc.psum_tensor(f"bank{i}", [P, 512], F32)) for i in range(8)]
        QB, TB, SB, PB, OB = banks[0:2], banks[2], banks[3:5], banks[5:7], banks[7]

        COUNTS = {
            "xs_hi": (2, 0),
            "xs_ready": (1, 0),
            "qkv_done": (12, 16),
            "squared": (8, 0),
            "v_kept": (4, 4),
            "rotated": (8, 8),
            "summed": (8, 2),
            "guarded": (2, 0),
            "ln_done": (2, 0),
            "seeded": (2, 0),
            "newton": (4, 0),
            "normed": (2, 2),
            "qk_added": (8, 2),
            "qk_scaled": (8, 8),
            "qkT_done": (8, 8),
            "qkT_kept": (8, 1),
            "s_done": (16, 0),
            "masked": (16, 2),
            "exp_done": (16, 2),
            "pT_done": (16, 4),
            "pT_kept": (16, 2),
            "pv_done": (16, 3),
            "recip_done": (4, 0),
            "o_kept": (4, 1),
            "oT_done": (4, 1),
            "oT_kept": (4, 0),
            "y_done": (1, 1),
            "x_updated": (1, 1),
            "f_shifted": (1, 0), "f_t1": (1, 1), "f_stats": (4, 0), "f_chain": (16, 0), "f_normed": (1, 0),
            "f_t2": (1, 0), "f_xn": (1, 0), "f_hi": (1, 0), "f_split": (1, 0), "f_w1": (6, 6),
            "f_gelu": (3, 0), "f_gated": (3, 3), "f_w2": (1, 1), "f_x": (1, 1),
        }
        S = {n: sem(n) for n in (*COUNTS, "phase", "loaded", "attn_loaded", "ffn_loaded", "stored", "lane0", "lane1", "lane2", "lane3", "prep", "prep_ffn", "o_copied", "o_t", "o_sum", "zeroed", "waited")}

        class Pass:

            def __init__(self, e, value, offset=0, known=None):
                self.e, self.value, self.offset = e, value, offset
                self.known = {} if known is None else known

            def __add__(self, n):
                return Pass(self.e, self.value, self.offset + n, self.known)

            def times(self, per):
                if per not in self.known:
                    self.known[per] = self.e.snap(self.value * per)
                return self.known[per]

        def wait(e, name, g, k):
            per, ahead = COUNTS[name]
            e.wait_ge(S[name], g.times(per) + (g.offset * per + ahead + k))

        def apart(e):
            e.sem_inc(S["waited"], 1)

        def give_ahead(e):
            for n, (_, ahead) in COUNTS.items():
                if ahead:
                    e.sem_inc(S[n], ahead)
            for n in ("lane0", "lane1", "lane2", "lane3", "o_t", "o_sum"):
                e.sem_inc(S[n], 1)
            e.sem_inc(S["phase"], PHASE_AHEAD)

        ENGINES = 4

        MEETINGS = 4
        PHASE_AHEAD = ENGINES + 1

        def meet(e, number):
            e.drain().then_inc(S["phase"], 1)
            e.wait_ge(S["phase"], number * ENGINES + PHASE_AHEAD)
            apart(e)

        block = ctx.enter_context(nc.Block())

        LANES = 4
        A_w = w1_raw[:, 0:3 * P]
        A_wp = w1_raw[:, 3 * P:4 * P]
        A_bp = w1_raw[:, 4 * P:5 * P]
        A_gb = w1_raw[:, 5 * P:5 * P + 2 * DH1]
        WIDE = H1 * W1N
        flat = lambda x: (x.rearrange("p a b c -> p (a b c)") if len(x.shape) == 4
                          else x.rearrange("p a b -> p (a b)"))
        lane_large = [flat(x) for x in (qT[:, :, :, :], kT[:, :, :, :], V[:, :, :, :], qk[:, :, :])]
        lane_small = [flat(x) for x in (tc[:, :, :], ts[:, :, :], sq[:, :, :], oT[:, 0:4, :])]
        lane_stats = flat(SM[:, :, :])

        vec_half = sb("vec_half", [P, 1])

        def bc(ap, n, inner):
            return ap.rearrange("p (n o) -> p n o", o=1).broadcast_to([P, n, inner])

        def rep(ap, n, inner):
            return ap.rearrange("p (o d) -> p o d", o=1).broadcast_to([P, n, inner])

        def h3(ap, d):
            return ap.rearrange("p (n d) -> p n d", d=d)

        V_ = nc.vector
        T_ = nc.tensor
        A_ = nc.scalar

        def mm(out, lhsT, rhs, start=True, stop=True, **k):
            return T_.matmul(out, lhsT, rhs, start=start, stop=stop, **k)

        def tr(out, in_, idn=None):
            return T_.transpose(out, in_, ident if idn is None else idn)

        stats_steps = []

        def lane_steps(lane):
            large, small_ = lane_large[lane], lane_small[lane]
            bank_a, bank_b = banks[2 * lane:2 * lane + 2]
            pair = (bank_a, bank_b)
            A_KX = large[:, 0:2 * WIDE].rearrange("p (w k) -> p w k", w=2)
            A_S = large[:, 2 * WIDE:3 * WIDE]
            A_PT = A_S
            A_P = large[:, 3 * WIDE:4 * WIDE]
            A_xn, A_xnT = A_P[:, 0:P], A_P[:, P:2 * P]
            A_qk, A_qk2, A_sq = (A_P[:, 2 * P * k:2 * P * (k + 1)] for k in (1, 2, 3))
            A_V = small_[:, 0:2 * P]
            A_twice = small_[:, 2 * P:4 * P]
            A_o, A_oT, A_z, A_qT = (small_[:, k * P:(k + 1) * P] for k in (4, 5, 6, 7))
            st = lane_stats[:, lane * 144:(lane + 1) * 144]
            st6, mv, rs1, tmp1 = st[:, 0:6], st[:, 6:8], st[:, 8:9], st[:, 9:10]
            mean, var, inv = (st[:, 16 + 32 * k:48 + 32 * k] for k in range(3))
            rsum1, rden1 = st[:, 112:128], st[:, 128:144]

            def layernorm_steps(src, dst):
                two = (lambda i: V_.bn_stats(st6, src(i)), lambda i: V_.bn_aggr(mv, st6))
                stats_steps.extend(two)
                return [
                    ("dve", two[0]),
                    ("dve", two[1]),
                    ("dve", lambda i: V_.tensor_scalar(mv[:, 1:2], mv[:, 1:2], LN_EPS, None, ALU.add)),
                    *rsqrt_steps(mv[:, 1:2], tmp1, rs1),
                    ("dve", lambda i: V_.tensor_scalar(dst, src(i), mv[:, 0:1], rs1, ALU.subtract, ALU.mult)),
                ]

            def rsqrt_steps(v, tmp, y):
                return [
                    ("act", lambda i: nc.scalar.activation(tmp, v, ACT.Ln, scale=LN_IN_SCALE)),
                    ("act", lambda i: nc.scalar.activation(y, tmp, ACT.Exp, scale=-0.5, bias=vec_half[:, 0:1])),
                    ("dve", lambda i: nc.vector.scalar_tensor_tensor(tmp, v, -0.5, y, ALU.mult, ALU.mult)),
                    ("dve", lambda i: nc.vector.tensor_tensor(tmp, tmp, y, ALU.mult)),
                    ("dve", lambda i: nc.vector.scalar_tensor_tensor(y, tmp, 1.5, y, ALU.add, ALU.mult)),
                ]

            def project_qkv(i):
                mm(bank_a[:, 0:2 * P], A_xnT, A_w[:, 0:2 * P])
                for w in range(2):
                    last = mm(bank_b[:, w * P:(w + 1) * P], A_twice[:, w * P:(w + 1) * P], A_w[:, 2 * P:3 * P])
                return last

            def scores1(i):
                for w in range(2):
                    for half in range(2):
                        last = mm(pair[half][w * W1N:(w + 1) * W1N, :], A_qT[:, w * W1N:(w + 1) * W1N],
                                  A_KX[:, w, half * 512:(half + 1) * 512])
                return last

            def transpose_p(half):
                def f(i):
                    for t in range(4):
                        last = tr(pair[half][:, t * P:(t + 1) * P], A_P[:, (4 * half + t) * P:(4 * half + t + 1) * P])
                    return last
                return f

            def pv1(i):
                for t in range(8):
                    for w in range(2):
                        last = mm(bank_a[w * W1N:(w + 1) * W1N, t * 16:(t + 1) * 16],
                                  A_PT[:, t * P + w * W1N:t * P + (w + 1) * W1N],
                                  A_V[:, w * P + t * 16:w * P + (t + 1) * 16])
                return last

            n32 = 2 * H1
            s = []
            s += layernorm_steps(lambda i: X1[:, i, :], A_xn)
            s.append(("pe", lambda i: tr(bank_b[:, 0:P], A_xn)))
            s.append(("act", lambda i: A_.activation(A_xnT, bank_b[:, 0:P], ACT.Copy)))
            s.append(("act", lambda i: A_.activation(
                A_twice.rearrange("p (w r t) -> p w r t", w=2, r=2),
                bank_b[:, 0:P].rearrange("p (w o t) -> p w o t", w=2, o=1).broadcast_to([P, 2, 2, W1N]), ACT.Copy)))
            s.append(("pe", project_qkv))
            s.append(("dve", lambda i: V_.tensor_tensor(h3(A_V, P), h3(bank_b[:, 0:2 * P], P), rep(parity, 2, P), ALU.mult)))
            s.append(("dve", lambda i: V_.tensor_reduce(mean, h3(bank_a[:, 0:2 * P], DH1), axis=AX.X, op=ALU.add)))
            s.append(("dve", lambda i: V_.tensor_scalar(mean, mean, 1.0 / DH1, None, ALU.mult)))
            s.append(("dve", lambda i: V_.tensor_tensor(h3(A_qk, DH1), h3(bank_a[:, 0:2 * P], DH1), bc(mean, n32, DH1), ALU.subtract)))
            s.append(("dve", lambda i: V_.tensor_tensor(A_sq, A_qk, A_qk, ALU.mult)))
            s.append(("dve", lambda i: V_.tensor_reduce(var, h3(A_sq, DH1), axis=AX.X, op=ALU.add)))
            s.append(("dve", lambda i: V_.tensor_scalar(var, var, 1.0 / DH1, LN_EPS, ALU.mult, ALU.add)))
            s += rsqrt_steps(var, mean, inv)
            s.append(("dve", lambda i: V_.tensor_tensor(h3(A_qk2, DH1), h3(A_qk, DH1), bc(inv, n32, DH1), ALU.mult)))
            s.append(("dve", lambda i: V_.tensor_tensor(h3(A_qk, DH1), h3(A_qk2, DH1), rep(A_gb[:, 0:DH1], n32, DH1), ALU.mult)))
            s.append(("dve", lambda i: V_.tensor_tensor(h3(A_qk2, DH1), h3(A_qk, DH1), rep(A_gb[:, DH1:2 * DH1], n32, DH1), ALU.add)))
            s.append(("pe", lambda i: (tr(bank_b[:, 0:P], A_qk2[:, 0:P]), tr(bank_a[:, 0:P], A_qk2[:, P:2 * P]))[1]))
            s.append(("act", lambda i: A_.activation(A_qT, bank_b[:, 0:P], ACT.Copy)))
            for w in range(2):
                s.append(("dve", lambda i, w=w: V_.tensor_tensor(
                    h3(A_KX[:, w, :], W1N), rep(bank_a[:, w * W1N:(w + 1) * W1N], H1, W1N), bc(head_mask, H1, W1N), ALU.mult)))
            s.append(("pe", scores1))
            for half in range(2):
                hh = slice(half * 8, half * 8 + 8)
                s.append(("dve", lambda i, half=half, hh=hh: V_.tensor_reduce(rsum1[:, hh], h3(pair[half][:, :], W1N), axis=AX.X, op=ALU.max)))
            for half in range(2):
                hh = slice(half * 8, half * 8 + 8)
                s.append(("dve", lambda i, half=half, hh=hh: V_.tensor_tensor(
                    h3(A_S[:, half * 512:(half + 1) * 512], W1N), h3(pair[half][:, :], W1N), bc(rsum1[:, hh], 8, W1N), ALU.subtract)))
            s.append(("act", lambda i: A_.activation(A_P, A_S, ACT.Exp)))
            s.append(("dve", lambda i: V_.tensor_reduce(rsum1, h3(A_P, W1N), axis=AX.X, op=ALU.add)))
            s.append(("dve", lambda i: V_.reciprocal(rden1, rsum1)))
            for half in range(2):
                s.append(("pe", transpose_p(half)))
                s.append(("act", lambda i, half=half: A_.activation(A_PT[:, half * 512:(half + 1) * 512], pair[half][:, :], ACT.Copy)))
            s.append(("pe", pv1))
            s.append(("dve", lambda i: V_.tensor_tensor(h3(A_o, DH1), h3(bank_a[:, 0:P], DH1), bc(rden1, H1, DH1), ALU.mult)))
            s.append(("pe", lambda i: tr(bank_b[:, 0:P], A_o)))
            s.append(("act", lambda i: A_.activation(A_oT, bank_b[:, 0:P], ACT.Copy)))
            s.append(("pe", lambda i: mm(bank_a[:, 0:P], A_oT, A_wp)))
            s.append(("dve", lambda i: V_.tensor_tensor(A_xn, X1[:, i, :], A_bp, ALU.add)))
            s.append(("dve", lambda i: V_.tensor_tensor(X1[:, i, :], bank_a[:, 0:P], A_xn, ALU.add)))
            s += layernorm_steps(lambda i: X1[:, i, :], A_z)
            s.append(("pe", lambda i: tr(bank_b[:, 0:P], A_z)))
            s.append(("act", lambda i: A_.activation(xT[:, bass.ds(i * P, P)], bank_b[:, 0:P], ACT.Copy)))
            return s

        def stage1(e, who):
            lanes = [lane_steps(lane) for lane in range(LANES)]
            n = len(lanes[0])
            with e.Fori(0, TILES // LANES) as i:
                tile = [e.snap(i * LANES + lane) for lane in range(LANES)]
                for k in range(n):
                    for lane, steps in enumerate(lanes):
                        engine, step = steps[k]
                        if engine == who:
                            e.wait_ge(S[f"lane{lane}"], i * n + (k + 1))
                            if step in stats_steps:
                                apart(e)
                            step(tile[lane]).then_inc(S[f"lane{lane}"], 1)

        QUNITS = [(b, u) for b in range(BLOCKS) for u in range(NQK)]
        VUNITS = [(b, v) for b in range(BLOCKS) for v in range(NV)]
        NQ = len(QUNITS)
        ORDER = {0: ("q", 0), 1: ("v", 0), 2: ("q", 1), 3: ("v", 1), 4: ("q", 2), 5: ("v", 2), 6: ("q", 3),
                 7: ("v", 3), 8: ("q", 4), 10: ("q", 5), 12: ("q", 6), 14: ("q", 7)}
        UNITS = list(ORDER.values())
        SEED_STEP = {7: 0, 15: 1}
        NEWTON_STEP = {8: 0, 16: 1}
        SCALE_STEP = {8: (0, 1), 9: (2, 3), 16: (4, 5), 17: (6, 7)}
        T_STEP = {10: (0,), 11: (1,), 12: (2,), 13: (3,), 18: (4,), 19: (5,), 20: (6,), 21: (7,)}
        SPLIT_STEP = 16
        Y_STEP = {1: (0, 1), 2: (2, 3), 3: (4, 5), 4: (6, 7)}
        X_STEP = 5
        EXP_LAG, T_LAG, KEEP_LAG, PV_LAG = 1, 2, 3, 4
        O_STEP = {OH * k + OH - 1 + PV_LAG + 1: k for k in range(OBATCHES)}
        OT_STEP = {n + 1: k for n, k in O_STEP.items()}
        STEPS = max(OT_STEP) + 1
        TB_USES = [("y", 0)] + [use for n in range(STEPS) for use in
                                [("qk", j) for j in T_STEP.get(n, ())] + [("o", OT_STEP[k]) for k in (n,) if k in OT_STEP]]

        def tb_free(e, use, g, b, a, y):
            for kind, i in reversed(TB_USES[:TB_USES.index(use)]):
                if kind == "y" and y:
                    return wait(e, "x_updated", g, 0)
                if kind == "qk" and a:
                    return wait(e, "qkT_kept", g + 1, i + 1)
                if kind == "o" and b:
                    return wait(e, "oT_kept", g, i + 1)
            if b:
                wait(e, "qkT_kept", g, NQ)
                if y:
                    wait(e, "oT_kept", g, 0)
        G_ = nc.gpsimd

        def a_pe(e, n, g, p, b_on, y):
            if n == 0:
                wait(e, "xs_ready", g, 1)
            if n in ORDER:
                kind, i = ORDER[n]
                m = UNITS.index((kind, i))
                back = 0 if m >= 2 else 1
                bkind, bi = UNITS[m - 2]
                if bkind == "q":
                    wait(e, "rotated", g, bi + 1 - back * NQ)
                else:
                    wait(e, "v_kept", g, bi + 1 - back * len(VUNITS))
                b, u = QUNITS[i] if kind == "q" else (VUNITS[i][0], NQK + VUNITS[i][1])
                high, low = (x[:, p, b * P:(b + 1) * P] for x in (xs_h, xs_l))
                cols = slice(u * UNIT, (u + 1) * UNIT)
                bank = QB[m % 2]
                mm(bank[:, :], high, wq_h[:, cols], True, False)
                mm(bank[:, :], low, wq_h[:, cols], False, False)
                mm(bank[:, :], high, wq_l[:, cols], False, True).then_inc(S["qkv_done"], 1)
            for j in T_STEP.get(n, ()):
                wait(e, "qk_scaled", g, j + 1)
                tb_free(e, ("qk", j), g + -1, b_on, True, y)
                for t in range(4):
                    last = tr(TB[:, t * P:(t + 1) * P], qk[:, j, t * P:(t + 1) * P])
                last.then_inc(S["qkT_done"], 1)

        def a_act(e, n, g, p):
            if n in ORDER:
                kind, i = ORDER[n]
                m = UNITS.index((kind, i))
                wait(e, "qkv_done", g, m + 1)
                if kind == "q":
                    wait(e, "summed", g, i - 1)
                    A_.activation(sq[:, i % 2, :], QB[m % 2][:, :], ACT.Square).then_inc(S["squared"], 1)
                else:
                    b, v = VUNITS[i]
                    A_.activation(V[:, p, b, v * UNIT:(v + 1) * UNIT], QB[m % 2][:, :],
                                  ACT.Copy).then_inc(S["v_kept"], 1)
            if n in SEED_STEP:
                b = SEED_STEP[n]
                wait(e, "guarded", g, b + 1)
                wait(e, "normed", g, b)
                A_.activation(rnt[:, :], ss[:, b, :], ACT.Ln, scale=LN_IN_SCALE).then_inc(S["ln_done"], 1)
                wait(e, "ln_done", g, b + 1)
                A_.activation(rn0[:, :], rnt[:, :], ACT.Exp, scale=-0.5,
                              bias=vec_half[:, 0:1]).then_inc(S["seeded"], 1)
            for j in T_STEP.get(n, ()):
                b, u = QUNITS[j]
                wait(e, "qkT_done", g, j + 1)
                dst = (qT if u < NQK // 2 else kT)[:, p, (u % 2) * 4:(u % 2) * 4 + 4, b * P:(b + 1) * P]
                A_.activation(dst, TB[:, :].rearrange("p (t c) -> p t c", t=4),
                              ACT.Copy).then_inc(S["qkT_kept"], 1)

        def a_dve(e, n, g, p):
            if n in ORDER and ORDER[n][0] == "q":
                i = ORDER[n][1]
                m = UNITS.index(ORDER[n])
                b, u = QUNITS[i]
                kind = 0 if u < NQK // 2 else 2
                bank = QB[m % 2]
                wait(e, "squared", g, i + 1)
                wait(e, "qk_added", g, i - 1)
                V_.tensor_tensor(h3(tc[:, i % 2, :], DH), h3(bank[:, :], DH), rep(tab[:, kind, b, :], UH, DH), ALU.mult)
                halves = dict(a=2, c=DH // 2)
                swapped = bank[:, :].rearrange("p (h a c) -> p h a c", **halves)[:, :, ::-1, :]
                sines = tab[:, kind + 1, b, :].rearrange("p (o a c) -> p o a c", o=1, a=2).broadcast_to([P, UH, 2, DH // 2])
                V_.tensor_tensor(ts[:, i % 2, :].rearrange("p (h a c) -> p h a c", **halves),
                                 swapped, sines, ALU.mult).then_inc(S["rotated"], 1)
                V_.tensor_reduce(ss[:, b, u * UH:(u + 1) * UH], h3(sq[:, i % 2, :], DH), axis=AX.X,
                                 op=ALU.add).then_inc(S["summed"], 1)
                if u == NQK - 1:
                    wait(e, "summed", g, i + 1)
                    V_.tensor_scalar(ss[:, b, :], ss[:, b, :], 1e-24, None, ALU.max).then_inc(S["guarded"], 1)
            if n in NEWTON_STEP:
                b = NEWTON_STEP[n]
                wait(e, "seeded", g, b + 1)
                V_.scalar_tensor_tensor(rnt[:, :], ss[:, b, :], -0.5, rn0[:, :], ALU.mult,
                                        ALU.mult).then_inc(S["newton"], 1)
                wait(e, "newton", g, 2 * b + 1)
                V_.tensor_tensor(rnt[:, :], rnt[:, :], rn0[:, :], ALU.mult).then_inc(S["newton"], 1)
                wait(e, "newton", g, 2 * b + 2)
                wait(e, "qk_scaled", g, 4 * b + 4 - NQ)
                V_.scalar_tensor_tensor(rn[:, b, :], rnt[:, :], 1.5, rn0[:, :], ALU.add,
                                        ALU.mult).then_inc(S["normed"], 1)

        def a_pool(e, n, g):
            if n in ORDER and ORDER[n][0] == "q":
                i = ORDER[n][1]
                wait(e, "rotated", g, i + 1)
                wait(e, "qkT_done", g, i + 1 - NQ)
                G_.tensor_tensor(qk[:, i, :], tc[:, i % 2, :], ts[:, i % 2, :], ALU.add).then_inc(S["qk_added"], 1)
            for j in SCALE_STEP.get(n, ()):
                b, u = QUNITS[j]
                wait(e, "normed", g, b + 1)
                wait(e, "qk_added", g, j + 1)
                G_.tensor_tensor(h3(qk[:, j, :], DH), h3(qk[:, j, :], DH),
                                 bc(rn[:, b, u * UH:(u + 1) * UH], UH, DH), ALU.mult).then_inc(S["qk_scaled"], 1)

        def b_pe(e, n, g, p):
            if n < HEADS:
                r = (n % 2) * DH
                if n == 0:
                    wait(e, "qkT_kept", g, NQ)
                    wait(e, "v_kept", g, len(VUNITS))
                wait(e, "masked", g, n - 1)
                q, k = qT[r:r + DH, p, n // 2, :], kT[r:r + DH, p, n // 2, :]
                mm(SB[n % 2][:, 0:P], q[:, 0:P], k[:, 0:P])
                mm(SB[n % 2][:, P:SW], q[:, P:LEN], k[:, P - WIN:LEN]).then_inc(S["s_done"], 1)

        def b_pe_late(e, n, g, p, a, y):
            h = n - T_LAG
            if 0 <= h < HEADS:
                wait(e, "exp_done", g, h + 1)
                wait(e, "pT_kept", g, h - 1)
                pr, bank = Pr[:, h % NP_, :], PB[h % 2]
                tr(bank[:, 0:P], pr[:, 0:P])
                tr(bank[:, P:KEYS1], pr[0:WIN, P:2 * P], ident[0:WIN, 0:WIN])
                tr(bank[:, KEYS1:SW], pr[:, 2 * P:3 * P]).then_inc(S["pT_done"], 1)
            h = n - PV_LAG
            if 0 <= h < HEADS:
                wait(e, "pT_kept", g, h + 1)
                if h % OH == 0:
                    wait(e, "o_kept", g, h // OH)
                v = [V[:, p, b, h * DH:(h + 1) * DH] for b in range(BLOCKS)]
                pt = PT[:, h % NT_, :]
                out = [OB[:, (b * OH + h % OH) * DH:(b * OH + h % OH + 1) * DH] for b in range(BLOCKS)]
                mm(out[0], pt[:, 0:P], v[0])
                mm(out[1], pt[:, KEYS1:SW], v[1], True, False, skip_group_check=True)
                mm(out[1][0:WIN, :], pt[:, P:KEYS1], v[0], False, True,
                   skip_group_check=True).then_inc(S["pv_done"], 1)
            if n in OT_STEP:
                k = OT_STEP[n]
                wait(e, "o_kept", g, k + 1)
                tb_free(e, ("o", k), g, True, a, y)
                for j in range(OH // 2):
                    for b in range(BLOCKS):
                        last = tr(TB[:, j * LEN + b * P:j * LEN + (b + 1) * P], osb[:, b, j * P:(j + 1) * P])
                last.then_inc(S["oT_done"], 1)

        def y_pe(e, n, g, a=True):
            for j in Y_STEP.get(n, ()):
                if j == 0:
                    wait(e, "oT_kept", g, OBATCHES)
                    if a:
                        wait(e, "qkT_kept", g + 1, NQ)
                last = mm(TB[:, 0:LEN], wo_sb[:, j, :], oT[:, j, :], j == 0, j == PAIRS - 1, skip_group_check=True)
                if j == PAIRS - 1:
                    last.then_inc(S["y_done"], 1)

        def y_dve(e, g, at):
            wait(e, "y_done", g, 1)
            V_.tensor_tensor(xT[:, bass.ds(at, LEN)], TB[:, 0:LEN], xT[:, bass.ds(at, LEN)],
                             ALU.add).then_inc(S["x_updated"], 1)

        def b_dve(e, n, g):
            if n < HEADS:
                wait(e, "s_done", g, n + 1)
                wait(e, "exp_done", g, n - 1)
                apart(e)
                for b, (lo, hi) in enumerate(((0, P), (P, SW))):
                    last = V_.tensor_tensor_reduce(
                        out=SM[:, n % 2, lo:hi], in0=SB[n % 2][:, lo:hi], in1=mask[:, lo:hi], scale=1.0,
                        scalar=NEG, op0=ALU.add, op1=ALU.min, accum_out=nmax[:, n, b:b + 1])
                last.then_inc(S["masked"], 1)

            h = n - KEEP_LAG
            if 0 <= h < HEADS:
                wait(e, "pT_done", g, h + 1)
                wait(e, "pv_done", g, h + 1 - NT_)
                V_.tensor_copy(PT[:, h % NT_, :], PB[h % 2][:, 0:SW]).then_inc(S["pT_kept"], 1)
            if n in O_STEP:
                k = O_STEP[n]
                heads = slice(k * OH, (k + 1) * OH)
                wait(e, "exp_done", g, (k + 1) * OH)
                V_.reciprocal(rden[:, :, heads], rsum[:, :, heads]).then_inc(S["recip_done"], 1)
                wait(e, "pv_done", g, (k + 1) * OH)
                wait(e, "oT_done", g, k)
                wait(e, "recip_done", g, k + 1)
                V_.tensor_tensor(osb[:, :, :].rearrange("p b (h d) -> p b h d", d=DH),
                                 OB[:, :].rearrange("p (b h d) -> p b h d", b=BLOCKS, d=DH),
                                 rden[:, :, heads].rearrange("p b (h o) -> p b h o", o=1)
                                 .broadcast_to([P, BLOCKS, OH, DH]), ALU.mult).then_inc(S["o_kept"], 1)

        def b_act(e, n, g):
            h = n - EXP_LAG
            if 0 <= h < HEADS:
                wait(e, "masked", g, h + 1)
                wait(e, "pT_done", g, h + 1 - NP_)
                pr = Pr[:, h % NP_, :]
                A_.activation(pr[:, 0:P], SM[:, h % 2, 0:P], ACT.Exp, scale=-1.0, bias=nmax[:, h, 0:1],
                              accum_out=rsum[:, 0, h:h + 1])
                A_.activation(pr[:, P + ZP:], SM[:, h % 2, P:SW], ACT.Exp, scale=-1.0, bias=nmax[:, h, 1:2],
                              accum_out=rsum[:, 1, h:h + 1]).then_inc(S["exp_done"], 1)

        def b_act_late(e, n, g):
            if n in OT_STEP:
                k = OT_STEP[n]
                wait(e, "oT_done", g, k + 1)
                wait(e, "y_done", g, 0)
                A_.activation(oT[:, k * OH // 2:(k + 1) * OH // 2, :].rearrange("p j t -> p (j t)"), TB[:, :],
                              ACT.Copy).then_inc(S["oT_kept"], 1)

        def split_act(e, g, p, at):
            wait(e, "qkv_done", g, -12)
            A_.activation(xs_h[0:64, p, :], xT[0:64, bass.ds(at, LEN)], ACT.Copy).then_inc(S["xs_hi"], 1)
            A_.activation(xs_h[64:P, p, 1:LEN], xT[64:P, bass.ds(at, LEN - 1)], ACT.Copy).then_inc(S["xs_hi"], 1)

        def split_dve(e, g, p, at):
            wait(e, "xs_hi", g, 2)
            V_.tensor_tensor(xs_l[0:64, p, :], xT[0:64, bass.ds(at, LEN)],
                             xs_h[0:64, p, :].bitcast(F32), ALU.subtract)
            V_.tensor_tensor(xs_l[64:P, p, 1:LEN], xT[64:P, bass.ds(at, LEN - 1)],
                             xs_h[64:P, p, 1:LEN].bitcast(F32), ALU.subtract).then_inc(S["xs_ready"], 1)

        def pass_pe(e, g, p, at, y, b, a, x):
            for n in range(STEPS):
                if b:
                    b_pe(e, n, g, p)
                if a:
                    a_pe(e, n, g + 1, 1 - p, b, y)
                if y:
                    y_pe(e, n, g + -1)
                if b:
                    b_pe_late(e, n, g, p, a, y)

        def pass_act(e, g, p, at, y, b, a, x):
            for n in range(STEPS):
                if b:
                    b_act(e, n, g)
                if a:
                    a_act(e, n, g + 1, 1 - p)
                if x and n == SPLIT_STEP:
                    split_act(e, g + 2, p, at + 2 * LEN)
                if b:
                    b_act_late(e, n, g)

        def pass_dve(e, g, p, at, y, b, a, x):
            for n in range(STEPS):
                if b:
                    b_dve(e, n, g)
                if a:
                    a_dve(e, n, g + 1, 1 - p)
                if y and n == X_STEP:
                    y_dve(e, g + -1, at - LEN)
                if x and n == SPLIT_STEP:
                    split_dve(e, g + 2, p, at + 2 * LEN)

        def pass_pool(e, g, p, at, y, b, a, x):
            if a:
                for n in range(STEPS):
                    a_pool(e, n, g + 1)

        def attention(e, layer, one_pass, split, project):
            first = Pass(e, e.snap(layer * SEQS))
            if split:
                split(e, first, 0, 0)
            one_pass(e, first + -1, 1, -LEN, False, False, True, True)
            one_pass(e, first, 0, 0, False, True, True, True)
            with e.Fori(0, SEQS // 2 - 2) as i:
                g = Pass(e, e.snap(layer * SEQS + i * 2))
                at = e.snap(i * (2 * LEN))
                one_pass(e, g + 1, 1, at + LEN, True, True, True, True)
                one_pass(e, g + 2, 0, at + 2 * LEN, True, True, True, True)
            for n in range(SEQS - 3, SEQS):
                one_pass(e, first + n, n % 2, n * LEN, True, True, n < SEQS - 1, n < SEQS - 2)
            if project:
                project(e, first + (SEQS - 1))

        def last_projection_pe(e, g):
            for n in Y_STEP:
                y_pe(e, n, g, False)

        def last_projection_dve(e, g):
            y_dve(e, g, (SEQS - 1) * LEN)

        FT1, FT2, FW, FY = banks[0], banks[1], banks[2:6], banks[6]
        xf = qk[:, 0, :]
        xn = h3(qk[:, 1, :], P)
        xnf = qk[:, 2, :]
        f_h, f_l = (x[:, :, :].rearrange("p a b -> p (a b)") for x in (xs_h, xs_l))
        gate = qk[:, 3:6, :]
        hid = [sq[:, 0, :], sq[:, 1, :], tc[:, 0, :]]
        f_st = ts[:, 0, 0:24]
        f_mv = ts[:, 0, 32:40].rearrange("p (t c) -> p t c", c=2)
        f_v, f_y, f_t, f_i = (ts[:, 0, 48 + 8 * k:48 + 8 * k + 4] for k in range(4))
        NT = GROUP // P
        F_ORDER = [(j, k) for j in range(3) for k in (1, 0)]

        def f_pe_w1(e, g):
            wait(e, "f_split", g, 1)
            for m, (j, k) in enumerate(F_ORDER):
                lo, size = HTILE[j]
                if m < 4:
                    wait(e, "f_gated", g, 0)
                elif k:
                    wait(e, "f_gelu", g, j - 1)
                else:
                    wait(e, "f_gated", g, j - 1)
                c = slice(k * HID + lo, k * HID + lo + size)
                bank = FW[m % 4]
                mm(bank[0:size, :], w1_h[:, c], f_h, True, False)
                mm(bank[0:size, :], w1_l[:, c], f_h, False, False)
                mm(bank[0:size, :], w1_h[:, c], f_l, False, True).then_inc(S["f_w1"], 1)

        def f_pe_t1(e, g):
            wait(e, "f_shifted", g, 1)
            for t in range(NT):
                last = tr(FT1[:, t * P:(t + 1) * P], xf[:, t * P:(t + 1) * P])
            last.then_inc(S["f_t1"], 1)

        def f_pe_w2(e, g):
            wait(e, "f_x", g, 0)
            for j, (lo, size) in enumerate(HTILE):
                wait(e, "f_gated", g, j + 1)
                last = mm(FY[:, :], w2_sb[0:size, j, :], hid[j][0:size, :], j == 0, j == 2)
            last.then_inc(S["f_w2"], 1)

        def f_pe_t2(e, g):
            wait(e, "f_normed", g, 1)
            for t in range(NT):
                last = tr(FT2[:, t * P:(t + 1) * P], xn[:, t, :])
            last.then_inc(S["f_t2"], 1)

        def f_act_gelu(e, g):
            for j, (lo, size) in enumerate(HTILE):
                wait(e, "f_w1", g, 2 * j + 1)
                wait(e, "f_gated", g, j - 2)
                A_.activation(gate[0:size, j, :], FW[(2 * j) % 4][0:size, :], ACT.Gelu,
                              bias=vec[0:size, 5 + j:6 + j]).then_inc(S["f_gelu"], 1)

        def f_act_scale(e, g):
            wait(e, "f_t2", g, 1)
            A_.activation(xnf, FT2[:, :], ACT.Identity, scale=vec[:, 0:1], bias=vec[:, 1:2]).then_inc(S["f_xn"], 1)
            wait(e, "f_w1", g, 0)
            wait(e, "f_xn", g, 1)
            A_.activation(f_h, xnf, ACT.Copy).then_inc(S["f_hi"], 1)

        def f_dve_shift(e, g, at):
            wait(e, "f_t1", g, 0)
            V_.tensor_copy(xf[0:64, :], xT[0:64, bass.ds(at, GROUP)])
            two = dict(a=2, c=LEN)
            V_.tensor_copy(xf[64:P, :].rearrange("p (a c) -> p a c", **two)[:, :, 1:],
                           xT[64:P, bass.ds(at, GROUP)].rearrange("p (a c) -> p a c", **two)[:, :, 0:LEN - 1]
                           ).then_inc(S["f_shifted"], 1)

        def f_dve_norm(e, g):
            wait(e, "f_t1", g, 1)
            apart(e)
            for t in range(NT):
                last = V_.bn_stats(f_st[:, 6 * t:6 * t + 6], FT1[:, t * P:(t + 1) * P])
                last.then_inc(S["f_stats"], 1)
            wait(e, "f_stats", g, NT)
            apart(e)
            n = 0

            def chain(ins):
                nonlocal n
                n += 1
                ins.then_inc(S["f_chain"], 1)
                wait(e, "f_chain", g, n)
                if n < NT:
                    apart(e)

            for t in range(NT):
                chain(V_.bn_aggr(f_mv[:, t, :], f_st[:, 6 * t:6 * t + 6]))
            chain(V_.tensor_scalar(f_v, f_mv[:, :, 1], LN_EPS, None, ALU.add))
            chain(V_.tensor_scalar(f_i.bitcast(I32), f_v.bitcast(I32), 1, None, ALU.logical_shift_right))
            chain(V_.tensor_scalar(f_y.bitcast(I32), f_i.bitcast(I32), -1.0, 1597463007.0, ALU.mult, ALU.add))
            for _ in range(3):
                chain(V_.scalar_tensor_tensor(f_t, f_v, -0.5, f_y, ALU.mult, ALU.mult))
                chain(V_.tensor_tensor(f_t, f_t, f_y, ALU.mult))
                chain(V_.scalar_tensor_tensor(f_y, f_t, 1.5, f_y, ALU.add, ALU.mult))
            for t in range(NT):
                last = V_.tensor_scalar(xn[:, t, :], FT1[:, t * P:(t + 1) * P], f_mv[:, t, 0:1], f_y[:, t:t + 1],
                                        ALU.subtract, ALU.mult)
            last.then_inc(S["f_normed"], 1)
            assert n == COUNTS["f_chain"][0], n

        def f_dve_gate(e, g):
            for j, (lo, size) in enumerate(HTILE):
                wait(e, "f_w1", g, 2 * j + 2)
                wait(e, "f_gelu", g, j + 1)
                if j == 0:
                    wait(e, "f_w2", g, 0)
                V_.scalar_tensor_tensor(hid[j][0:size, :], FW[(2 * j + 1) % 4][0:size, :], vec[0:size, 2 + j:3 + j],
                                        gate[0:size, j, :], ALU.add, ALU.mult).then_inc(S["f_gated"], 1)

        def f_dve_split(e, g):
            wait(e, "f_hi", g, 1)
            V_.tensor_tensor(f_l, xnf, f_h.bitcast(F32), ALU.subtract).then_inc(S["f_split"], 1)

        def f_dve_x(e, g, at):
            wait(e, "f_w2", g, 1)
            V_.scalar_tensor_tensor(xT[:, bass.ds(at, GROUP)], FY[:, :], vec[:, 8:9], xT[:, bass.ds(at, GROUP)],
                                    ALU.add, ALU.add).then_inc(S["f_x"], 1)

        def ffn_pe(e, g, at, b, a):
            if b:
                f_pe_w1(e, g)
            if a:
                f_pe_t1(e, g + 1)
            if b:
                f_pe_w2(e, g)
            if a:
                f_pe_t2(e, g + 1)

        def ffn_act(e, g, at, b, a):
            if b:
                f_act_gelu(e, g)
            if a:
                f_act_scale(e, g + 1)

        def ffn_dve(e, g, at, b, a):
            if a:
                f_dve_shift(e, g + 1, at + GROUP)
            if b:
                f_dve_gate(e, g)
            if a:
                f_dve_norm(e, g + 1)
            if b:
                f_dve_x(e, g, at)
            if a:
                f_dve_split(e, g + 1)

        def feed_forward(e, layer, one_pass):
            first = Pass(e, e.snap(layer * GROUPS))
            one_pass(e, first + -1, -GROUP, False, True)
            with e.Fori(0, GROUPS - 1) as i:
                at = e.snap(i * GROUP)
                one_pass(e, Pass(e, e.snap(layer * GROUPS + i)), at, True, True)
            one_pass(e, first + (GROUPS - 1), (GROUPS - 1) * GROUP, True, False)

        C3 = 3 * INNER
        CA = C3 // 2

        def prepare_act(e, layer):
            A_.preload_act_table_set("natural_log_exp_and_others")
            e.wait_ge(S["attn_loaded"], layer * 48 + 48)
            A_.activation(wq_h[:, 0:CA], wq_raw[:, 0:CA], ACT.Copy).then_inc(S["prep"], 1)
            A_.activation(wq_h[:, CA:], wq_raw[:, CA:], ACT.Copy).then_inc(S["prep"], 1)

        def prepare_dve(e, layer):
            for x in (xs_h, xs_l):
                V_.memset(x[64:P, :, 0:1].bitcast(F32), 0.0)
            e.wait_ge(S["attn_loaded"], layer * 48 + 48)
            swapped = [qks[:, i, :].rearrange("p (o a c) -> p o a c", o=1, a=2)[:, :, ::-1, :]
                       .broadcast_to([P, BLOCKS, 2, DH // 2]) for i in range(2)]
            for i in range(2):
                V_.tensor_tensor(tab[:, 2 * i, :, :], rot[:, 2 * i, :, :], rep(qks[:, i, :], BLOCKS, DH), ALU.mult)
                V_.tensor_tensor(tab[:, 2 * i + 1, :, :].rearrange("p b (a c) -> p b a c", a=2),
                                 rot[:, 2 * i + 1, :, :].rearrange("p b (a c) -> p b a c", a=2), swapped[i], ALU.mult)
            e.wait_ge(S["prep"], layer * 2 + 1)
            V_.tensor_tensor(wq_l[:, 0:CA], wq_raw[:, 0:CA], wq_h[:, 0:CA].bitcast(F32), ALU.subtract)

        def prepare_pool(e, layer):
            e.wait_ge(S["prep"], layer * 2 + 2)
            G_.tensor_tensor(wq_l[:, CA:], wq_raw[:, CA:], wq_h[:, CA:].bitcast(F32), ALU.subtract)

        def prepare_ffn_act(e, layer):
            e.wait_ge(S["ffn_loaded"], layer * 48 + 48)
            A_.activation(w1_h[:, :], w1_raw[:, :], ACT.Copy).then_inc(S["prep_ffn"], 1)

        def prepare_ffn_dve(e, layer):
            e.wait_ge(S["ffn_loaded"], layer * 48 + 48)
            V_.memset(xf[64:P, :].rearrange("p (a c) -> p a c", a=2)[:, :, 0:1], 0.0)
            e.wait_ge(S["prep_ffn"], layer + 1)
            V_.tensor_tensor(w1_l[:, :], w1_raw[:, :], w1_h[:, :].bitcast(F32), ALU.subtract)

        o_in = qk[:, 0, :]
        o_out = qk[:, 1:3, :]

        def finish(e, who):
            with e.Fori(0, GROUPS) as i:
                if who == "act":
                    e.wait_ge(S["o_t"], i + 1)
                    A_.activation(o_in, xT[:, bass.ds(i * GROUP, GROUP)], ACT.Copy).then_inc(S["o_copied"], 1)
                if who == "pe":
                    e.wait_ge(S["o_copied"], i + 1)
                    e.wait_ge(S["o_sum"], i + 1)
                    for t in range(NT):
                        last = tr(FT1[:, t * P:(t + 1) * P], o_in[:, t * P:(t + 1) * P])
                    last.then_inc(S["o_t"], 1)
                if who == "dve":
                    e.wait_ge(S["o_t"], i + 2)
                    V_.tensor_tensor(X1[:, bass.ds(i * NT, NT), :], X1[:, bass.ds(i * NT, NT), :],
                                     h3(FT1[:, :], P), ALU.add).then_inc(S["o_sum"], 1)

        def program(e, who, one_pass, split, project, prepare, one_ffn, prepare_ffn):
            stage1(e, who)
            meet(e, 1)
            with e.Fori(0, DEPTH) as layer:
                if prepare:
                    prepare(e, layer)
                meet(e, layer * MEETINGS + 2)
                attention(e, layer, one_pass, split, project)
                meet(e, layer * MEETINGS + 3)
                if prepare_ffn:
                    prepare_ffn(e, layer)
                meet(e, layer * MEETINGS + 4)
                if one_ffn:
                    feed_forward(e, layer, one_ffn)
                meet(e, layer * MEETINGS + 5)
            finish(e, who)

        @block.sync
        def _(sp):
            for dst, src in ((X1[:, :, :], x_in.rearrange("(t p) d -> p t d", p=P)), (small[:, :], c_small),
                             (w1_raw[:, 0:w_first.shape[1]], w_first),
                             (rot[:, :, :, :].rearrange("p a b c -> p (a b c)"), c_rot)):
                sp.dma_start(dst, src).then_inc(S["loaded"], 16)
            with sp.Fori(0, DEPTH) as layer:
                sp.wait_ge(S["phase"], layer * (MEETINGS * ENGINES) + 1)
                sp.dma_start(wq_raw[:, :], wqkv[layer, :, :]).then_inc(S["attn_loaded"], 16)
                sp.dma_start(wo_sb[:, :, :].rearrange("p a b -> p (a b)"), wo[layer, :, :]).then_inc(S["attn_loaded"], 16)
                sp.dma_start(qks[:, :, :].rearrange("p a b -> p (a b)"), qkscale[layer, :, :]).then_inc(S["attn_loaded"], 16)
                sp.wait_ge(S["phase"], layer * (MEETINGS * ENGINES) + ENGINES + PHASE_AHEAD)
                sp.dma_start(w1_raw[:, :], fw1[layer, :, :]).then_inc(S["ffn_loaded"], 16)
                sp.dma_start(w2_sb[:, :, :].rearrange("p a b -> p (a b)"), fw2[layer, :, :]).then_inc(S["ffn_loaded"], 16)
                sp.dma_start(vec[:, :], vectors[layer, :, :]).then_inc(S["ffn_loaded"], 16)
            o = out.rearrange("(t p) d -> p t d", p=P)
            for i in range(GROUPS):
                sp.wait_ge(S["o_sum"], i + 2)
                sp.dma_start(o[:, i * NT:(i + 1) * NT, :], X1[:, i * NT:(i + 1) * NT, :]).then_inc(S["stored"], 16)
            sp.wait_ge(S["stored"], 16 * GROUPS)

        @block.gpsimd
        def _(pool):
            give_ahead(pool)
            G_.memset(Pr[:, :, :], 0.0).then_inc(S["zeroed"], 1)
            G_.memset(vec_half[:, :], HALF_LOG).then_inc(S["zeroed"], 1)
            program(pool, "pool", pass_pool, None, None, prepare_pool, None, None)

        @block.scalar
        def _(act):
            act.wait_ge(S["loaded"], 64)
            act.wait_ge(S["zeroed"], 2)
            A_.preload_act_table_set("natural_log_exp_and_others")
            program(act, "act", pass_act, split_act, None, prepare_act, ffn_act, prepare_ffn_act)

        @block.vector
        def _(dve):
            dve.wait_ge(S["loaded"], 64)
            program(dve, "dve", pass_dve, split_dve, last_projection_dve, prepare_dve, ffn_dve, prepare_ffn_dve)

        @block.tensor
        def _(pe):
            pe.wait_ge(S["loaded"], 64)
            program(pe, "pe", pass_pe, None, last_projection_pe, None, ffn_pe, None)


def kernel(L0_attn_x, L0_attn_W_qkv, L0_attn_ln_gamma, L0_attn_ln_beta, L0_attn_W_proj, L0_attn_b_proj, L0_ffn_Wqkv,
           L0_ffn_q_scale, L0_ffn_k_scale, L0_ffn_Wo, L0_ffn_ln_g, L0_ffn_ln_b, L0_ffn_W1, L0_ffn_b1, L0_ffn_W2,
           L0_ffn_b2):
    import concourse.bacc as bacc
    from concourse.bass_utils import run_bass_kernel_spmd

    a = lambda x: np.ascontiguousarray(x)
    wide = lambda x: np.broadcast_to(a(x)[None, :], (P, x.shape[0]))
    first = np.concatenate([a(L0_attn_W_qkv), a(L0_attn_W_proj), wide(L0_attn_b_proj), wide(L0_attn_ln_gamma),
                            wide(L0_attn_ln_beta)], 1)
    scales = np.stack([a(L0_ffn_q_scale), a(L0_ffn_k_scale)], 1).reshape(DEPTH, 1, 2 * DH)
    w2 = np.zeros((DEPTH, 3 * P, DM), np.float32)
    w2[:, :HID] = a(L0_ffn_W2)
    vectors = np.zeros((DEPTH, P, 9), np.float32)
    vectors[:, :, 0], vectors[:, :, 1], vectors[:, :, 8] = a(L0_ffn_ln_g), a(L0_ffn_ln_b), a(L0_ffn_b2)
    for k in range(2):
        for j, (lo, size) in enumerate(HTILE):
            vectors[:, :size, 2 + 3 * k + j] = a(L0_ffn_b1)[:, k * HID + lo:k * HID + lo + size]
    c_rot, c_small = consts()
    arrays = {
        "x_in": a(L0_attn_x).reshape(TOKENS, DM),
        "w_first": first,
        "wqkv": a(L0_ffn_Wqkv),
        "wo": a(L0_ffn_Wo).reshape(DEPTH, PAIRS, P, DM).transpose(0, 2, 1, 3).reshape(DEPTH, P, PAIRS * DM),
        "qkscale": np.broadcast_to(scales, (DEPTH, P, 2 * DH)),
        "fw1": a(L0_ffn_W1),
        "fw2": w2.reshape(DEPTH, 3, P, DM).transpose(0, 2, 1, 3).reshape(DEPTH, P, 3 * DM),
        "vectors": vectors,
        "c_rot": c_rot,
        "c_small": c_small,
    }
    arrays = {k: np.ascontiguousarray(v) for k, v in arrays.items()}
    nc = bacc.Bacc("TRN2", target_bir_lowering=False, num_devices=1)
    args = [nc.dram_tensor(k, v.shape, mybir.dt.from_np(v.dtype), kind="ExternalInput").ap() for k, v in arrays.items()]
    out = nc.dram_tensor("out", (TOKENS, DM), F32, kind="ExternalOutput").ap()
    build(nc, *args, out)
    r = run_bass_kernel_spmd(nc, [arrays], core_ids=[0])
    return r.results[0]["out"].reshape(SEQS, LEN, DM)
```

```python
import numpy as np
import concourse.bass as bass
from concourse import mybir
from contextlib import ExitStack

F32 = mybir.dt.float32
F32R = mybir.dt.float32r
I32 = mybir.dt.int32
ALU = mybir.AluOpType
ACT = mybir.ActivationFunctionType
AX = mybir.AxisListType

P = 128
SEQS, LEN, DM = 16, 256, 128
TOKENS = SEQS * LEN
BLOCKS = LEN // P
TILES = TOKENS // P
W1N, H1, DH1 = 64, 16, 8
DEPTH, HEADS, DH, WIN = 6, 16, 64, 32
INNER = HEADS * DH
PAIRS = HEADS // 2
OH = 4
OBATCHES = HEADS // OH
UNIT = 512
UH = UNIT // DH
NQK = 2 * INNER // UNIT
NV = INNER // UNIT
KEYS1 = P + WIN
SW = P + KEYS1
QK_SCALE = 8.0
LN_EPS = 1e-5
HID = int(DM * 4 * 2 / 3)
HTILE = [(0, 128), (128, 128), (256, HID - 256)]
GROUP = 2 * LEN
GROUPS = TOKENS // GROUP
NEG = 3.0e38
LN_IN_SCALE = 65536.0
HALF_LOG = 5.545177444479562


def consts():
    half = np.arange(0, DH, 2, dtype=np.float32)
    inv_freq = (np.float32(1.0) / np.float32(10000.0) ** (half / np.float32(DH))).astype(np.float32)
    t = np.arange(LEN, dtype=np.float32)
    freqs = (t[:, None] * inv_freq[None, :]).astype(np.float32)
    freqs = np.concatenate([freqs, freqs], -1)
    base = (half + np.float32(0.4 * DH)) / np.float32(1.4 * DH)
    power = (t - LEN // 2) / np.float32(WIN // 2)
    scale = (base[None, :].astype(np.float32) ** power[:, None]).astype(np.float32)
    scale = np.concatenate([scale, scale], -1)
    sign = np.concatenate([-np.ones(DH // 2), np.ones(DH // 2)]).astype(np.float32)
    cos, sin = np.cos(freqs), np.sin(freqs)
    rot = np.stack([-QK_SCALE * cos * scale, -QK_SCALE * sin * scale * sign,
                    cos / scale, sin / scale * sign]).astype(np.float32)
    rot = rot.reshape(4, BLOCKS, P, DH).transpose(2, 0, 1, 3).copy()
    i = np.arange(P)[:, None]
    j0, j1 = np.arange(P)[None, :], np.arange(KEYS1)[None, :] - WIN
    mask = np.concatenate([np.where((i < j) | (i > j + WIN), NEG, 0.0) for j in (j0, j1)], 1)
    ident = np.eye(P)
    head_mask = (np.arange(P)[:, None] // DH1 == np.arange(H1)[None, :])
    parity = (np.arange(P)[:, None] // W1N == (np.arange(P)[None, :] // DH1) % 2)
    small = np.concatenate([mask, ident, head_mask, parity], 1).astype(np.float32)
    return rot.reshape(P, -1), small


def build(nc, x_in, w_first, wqkv, wo, qkscale, fw1, fw2, vectors, c_rot, c_small, out):
    ctx = ExitStack()
    with ctx:
        def sb(name, shape, dt=F32):
            return ctx.enter_context(nc.sbuf_tensor(name, shape, dt))

        def sem(name):
            return ctx.enter_context(nc.semaphore(name))

        X1 = sb("X1", [P, TILES, DM])
        xT = sb("xT", [P, TOKENS])
        rot = sb("rot", [P, 4, BLOCKS, DH])
        small = sb("small", [P, SW + P + H1 + P])
        mask = small[:, 0:SW]
        ident = small[:, SW:SW + P]
        head_mask = small[:, SW + P:SW + P + H1]
        parity = small[:, SW + P + H1:]
        wq_raw = sb("wq_raw", [P, 3 * INNER])
        wq_h = sb("wq_h", [P, 3 * INNER], F32R)
        wq_l = sb("wq_l", [P, 3 * INNER], F32R)
        wo_sb = sb("wo_sb", [P, PAIRS, DM])
        w1_raw = sb("w1_raw", [P, 2 * HID])
        w1_h = sb("w1_h", [P, 2 * HID], F32R)
        w1_l = sb("w1_l", [P, 2 * HID], F32R)
        w2_sb = sb("w2_sb", [P, 3, DM])
        vec = sb("vec", [P, 2 + 6 + 1])
        qks = sb("qks", [P, 2, DH])
        tab = sb("tab", [P, 4, BLOCKS, DH])
        xs_h = sb("xs_h", [P, 2, LEN], F32R)
        xs_l = sb("xs_l", [P, 2, LEN], F32R)
        sq = sb("sq", [P, 2, UNIT])
        tc = sb("tc", [P, 2, UNIT])
        ts = sb("ts", [P, 2, UNIT])
        qk = sb("qk", [P, BLOCKS * NQK, UNIT])
        ss = sb("ss", [P, BLOCKS, 2 * HEADS])
        rn0 = sb("rn0", [P, 2 * HEADS])
        rnt = sb("rnt", [P, 2 * HEADS])
        rn = sb("rn", [P, BLOCKS, 2 * HEADS])
        qT = sb("qT", [P, 2, PAIRS, LEN])
        kT = sb("kT", [P, 2, PAIRS, LEN])
        V = sb("V", [P, 2, BLOCKS, INNER])
        NP_ = 4
        SM = sb("SM", [P, 2, SW])
        nmax = sb("nmax", [P, HEADS, 2])
        rsum = sb("rsum", [P, BLOCKS, HEADS])
        rden = sb("rden", [P, BLOCKS, HEADS])
        ZP = P - WIN
        Pr = sb("Pr", [P, NP_, P + ZP + KEYS1])
        NT_ = 4
        PT = sb("PT", [P, NT_, SW])
        oraw = sb("oraw", [P, BLOCKS, OH * DH])
        osb = sb("osb", [P, BLOCKS, OH * DH])
        oT = sb("oT", [P, PAIRS, LEN])
        banks = [ctx.enter_context(nc.psum_tensor(f"bank{i}", [P, 512], F32)) for i in range(8)]
        QB, TB, SB, PB, OB = banks[0:2], banks[2], banks[3:5], banks[5:7], banks[7]

        COUNTS = {
            "xs_hi": (2, 0),
            "xs_ready": (1, 0),
            "qkv_done": (12, 16),
            "squared": (8, 0),
            "v_kept": (4, 4),
            "rotated": (8, 8),
            "summed": (8, 2),
            "guarded": (2, 0),
            "ln_done": (2, 0),
            "seeded": (2, 0),
            "newton": (4, 0),
            "normed": (2, 2),
            "qk_added": (8, 2),
            "qk_scaled": (8, 8),
            "qkT_done": (8, 8),
            "qkT_kept": (8, 1),
            "s_done": (16, 0),
            "masked": (16, 2),
            "exp_done": (16, 2),
            "pT_done": (16, 4),
            "pT_act": (8, 1),
            "pT_dve": (8, 1),
            "pv_done": (16, 4),
            "recip_done": (4, 0),
            "o_read": (4, 1),
            "o_divided": (4, 4),
            "oT_done": (4, 1),
            "oT_kept": (4, 0),
            "y_done": (1, 1),
            "x_updated": (1, 1),
            "f_shifted": (1, 0),
            "f_t1": (1, 2),
            "f_tok": (1, 2),
            "f_stats": (4, 0),
            "f_chain": (13, 0),
            "f_normed": (1, 0),
            "f_t2": (1, 2),
            "f_xn": (1, 1),
            "f_hi": (1, 0),
            "f_split": (1, 2),
            "f_w1": (6, 7),
            "f_gelu": (3, 3),
            "f_gated": (3, 3),
            "f_w2": (1, 2),
            "f_x": (1, 1),
        }
        S = {n: sem(n) for n in (*COUNTS, "phase", "loaded", "attn_loaded", "ffn_loaded", "stored", "lane0", "lane1", "lane2", "lane3", "prep", "prep_ffn", "w1_ready", "o_copied", "o_t", "o_sum", "zeroed", "waited")}

        class Pass:

            def __init__(self, e, value, offset=0, known=None):
                self.e, self.value, self.offset = e, value, offset
                self.known = {} if known is None else known

            def __add__(self, n):
                return Pass(self.e, self.value, self.offset + n, self.known)

            def times(self, per):
                if per not in self.known:
                    self.known[per] = self.e.snap(self.value * per)
                return self.known[per]

        def count(name, g, k):
            per, ahead = COUNTS[name]
            return g.times(per) + (g.offset * per + ahead + k)

        def apart(e):
            e.sem_inc(S["waited"], 1)

        def give_ahead(e):
            for n, (_, ahead) in COUNTS.items():
                if ahead:
                    e.sem_inc(S[n], ahead)
            for n in ("lane0", "lane1", "lane2", "lane3", "o_t", "o_sum"):
                e.sem_inc(S[n], 1)
            e.sem_inc(S["phase"], PHASE_AHEAD)

        ENGINES = 4

        MEETINGS = 3
        PHASE_AHEAD = ENGINES + 1

        def meet(e, number):
            e.drain().then_inc(S["phase"], 1)
            e.wait_ge(S["phase"], number * ENGINES + PHASE_AHEAD)
            apart(e)

        block = ctx.enter_context(nc.Block())

        LANES = 4
        w_qkv = w1_raw[:, 0:3 * P]
        w_proj = w1_raw[:, 3 * P:4 * P]
        bias_out = w1_raw[:, 4 * P:5 * P]
        gamma_beta = w1_raw[:, 5 * P:5 * P + 2 * DH1]
        WIDE = H1 * W1N
        flat = lambda x: (x.rearrange("p a b c -> p (a b c)") if len(x.shape) == 4
                          else x.rearrange("p a b -> p (a b)"))
        lane_large = [flat(x) for x in (qT[:, :, :, :], kT[:, :, :, :], V[:, :, :, :], qk[:, :, :])]
        lane_small = [flat(x) for x in (tc[:, :, :], ts[:, :, :], sq[:, :, :], oT[:, 0:4, :])]
        lane_stats = flat(SM[:, :, :])

        vec_half = sb("vec_half", [P, 1])

        def bc(ap, n, inner):
            return ap.rearrange("p (n o) -> p n o", o=1).broadcast_to([P, n, inner])

        def rep(ap, n, inner):
            return ap.rearrange("p (o d) -> p o d", o=1).broadcast_to([P, n, inner])

        def h3(ap, d):
            return ap.rearrange("p (n d) -> p n d", d=d)

        V_ = nc.vector
        T_ = nc.tensor
        A_ = nc.scalar
        G_ = nc.gpsimd

        def mm(out, lhsT, rhs, start=True, stop=True, **k):
            return T_.matmul(out, lhsT, rhs, start=start, stop=stop, **k)

        def tr(out, in_, idn=None):
            return T_.transpose(out, in_, ident if idn is None else idn)

        STAGE1_STEPS = (
            "statistics", "aggregate", "epsilon", "log", "seed", "newton1", "newton2", "newton3", "normalise",
            "transpose", "keep", "keep_twice", "project", "values", "sums", "means", "centre", "squares",
            "square_sums", "head_epsilon", "head_log", "head_seed", "head_newton1", "head_newton2", "head_newton3",
            "head_normalise", "gamma", "beta", "transpose_qk", "keep_q", "spread_k0", "spread_k1", "scores",
            "maximum0", "maximum1", "subtract0", "subtract1", "exp", "row_sums", "inverse_sums",
            "transpose_p0", "keep_p0", "transpose_p1", "keep_p1", "weigh_values", "divide", "transpose_o", "keep_o",
            "project_out", "add_bias", "residual", "statistics_2", "aggregate_2", "epsilon_2", "log_2", "seed_2",
            "newton1_2", "newton2_2", "newton3_2", "normalise_2", "transpose_2", "keep_2")
        N1 = len(STAGE1_STEPS)

        class Lane:

            def __init__(self, lane):
                large, small_ = lane_large[lane], lane_small[lane]
                self.number, self.done = lane, S[f"lane{lane}"]
                self.a, self.b = self.pair = banks[2 * lane:2 * lane + 2]
                self.kx = large[:, 0:2 * WIDE].rearrange("p (w k) -> p w k", w=2)
                self.s = large[:, 2 * WIDE:3 * WIDE]
                self.pt = self.s
                self.p = large[:, 3 * WIDE:4 * WIDE]
                self.xn, self.xnT = self.p[:, 0:P], self.p[:, P:2 * P]
                self.qk, self.qk2, self.sq = (self.p[:, 2 * P * k:2 * P * (k + 1)] for k in (1, 2, 3))
                self.v = small_[:, 0:2 * P]
                self.twice = small_[:, 2 * P:4 * P]
                self.o, self.oT, self.z, self.qT = (small_[:, k * P:(k + 1) * P] for k in (4, 5, 6, 7))
                st = lane_stats[:, lane * 144:(lane + 1) * 144]
                self.st6, self.mv, self.mu, self.variance = st[:, 0:6], st[:, 6:8], st[:, 6:7], st[:, 7:8]
                self.inverse, self.scratch = st[:, 8:9], st[:, 9:10]
                self.head_mean, self.head_var, self.head_inv = (st[:, 16 + 32 * k:48 + 32 * k] for k in range(3))
                self.rsum, self.rden = st[:, 112:128], st[:, 128:144]

        lanes = [Lane(lane) for lane in range(LANES)]
        NH = 2 * H1
        HALVES = [slice(0, H1 // 2), slice(H1 // 2, H1)]

        def stage1(e, engine):
            with e.Fori(0, TILES // LANES) as i:
                def before(step):
                    return i * N1 + (STAGE1_STEPS.index(step) + 1)

                engine(e, before, [e.snap(i * LANES + lane) for lane in range(LANES)])

        def root_act(e, before, v, scratch, y, log, seed):
            for L in lanes:
                e.wait_ge(L.done, before(log))
                A_.activation(scratch(L), v(L), ACT.Ln, scale=LN_IN_SCALE).then_inc(L.done, 1)
            for L in lanes:
                e.wait_ge(L.done, before(seed))
                A_.activation(y(L), scratch(L), ACT.Exp, scale=-0.5, bias=vec_half[:, 0:1]).then_inc(L.done, 1)

        def root_dve(e, before, v, scratch, y, steps):
            for L in lanes:
                e.wait_ge(L.done, before(steps[0]))
                V_.scalar_tensor_tensor(scratch(L), v(L), -0.5, y(L), ALU.mult, ALU.mult).then_inc(L.done, 1)
            for L in lanes:
                e.wait_ge(L.done, before(steps[1]))
                V_.tensor_tensor(scratch(L), scratch(L), y(L), ALU.mult).then_inc(L.done, 1)
            for L in lanes:
                e.wait_ge(L.done, before(steps[2]))
                V_.scalar_tensor_tensor(y(L), scratch(L), 1.5, y(L), ALU.add, ALU.mult).then_inc(L.done, 1)

        def layernorm_dve(e, before, tile, dst, suffix):
            for L in lanes:
                e.wait_ge(L.done, before("statistics" + suffix))
                apart(e)
                V_.bn_stats(L.st6, X1[:, tile[L.number], :]).then_inc(L.done, 1)
            for L in lanes:
                e.wait_ge(L.done, before("aggregate" + suffix))
                apart(e)
                V_.bn_aggr(L.mv, L.st6).then_inc(L.done, 1)
            for L in lanes:
                e.wait_ge(L.done, before("epsilon" + suffix))
                V_.tensor_scalar(L.variance, L.variance, LN_EPS, None, ALU.add).then_inc(L.done, 1)
            root_dve(e, before, lambda L: L.variance, lambda L: L.scratch, lambda L: L.inverse,
                     ["newton%d%s" % (k, suffix) for k in (1, 2, 3)])
            for L in lanes:
                e.wait_ge(L.done, before("normalise" + suffix))
                V_.tensor_scalar(dst(L), X1[:, tile[L.number], :], L.mu, L.inverse,
                                 ALU.subtract, ALU.mult).then_inc(L.done, 1)

        def stage1_dve(e, before, tile):
            layernorm_dve(e, before, tile, lambda L: L.xn, "")
            for L in lanes:
                e.wait_ge(L.done, before("values"))
                V_.tensor_tensor(h3(L.v, P), h3(L.b[:, 0:2 * P], P), rep(parity, 2, P), ALU.mult).then_inc(L.done, 1)
            for L in lanes:
                e.wait_ge(L.done, before("sums"))
                V_.tensor_reduce(L.head_mean, h3(L.a[:, 0:2 * P], DH1), axis=AX.X, op=ALU.add).then_inc(L.done, 1)
            for L in lanes:
                e.wait_ge(L.done, before("means"))
                V_.tensor_scalar(L.head_mean, L.head_mean, 1.0 / DH1, None, ALU.mult).then_inc(L.done, 1)
            for L in lanes:
                e.wait_ge(L.done, before("centre"))
                V_.tensor_tensor(h3(L.qk, DH1), h3(L.a[:, 0:2 * P], DH1), bc(L.head_mean, NH, DH1),
                                 ALU.subtract).then_inc(L.done, 1)
            for L in lanes:
                e.wait_ge(L.done, before("square_sums"))
                V_.tensor_reduce(L.head_var, h3(L.sq, DH1), axis=AX.X, op=ALU.add).then_inc(L.done, 1)
            for L in lanes:
                e.wait_ge(L.done, before("head_epsilon"))
                V_.tensor_scalar(L.head_var, L.head_var, 1.0 / DH1, LN_EPS, ALU.mult, ALU.add).then_inc(L.done, 1)
            root_dve(e, before, lambda L: L.head_var, lambda L: L.head_mean, lambda L: L.head_inv,
                     ["head_newton%d" % k for k in (1, 2, 3)])
            for L in lanes:
                e.wait_ge(L.done, before("head_normalise"))
                V_.tensor_tensor(h3(L.qk2, DH1), h3(L.qk, DH1), bc(L.head_inv, NH, DH1), ALU.mult).then_inc(L.done, 1)
            for L in lanes:
                e.wait_ge(L.done, before("gamma"))
                V_.tensor_tensor(h3(L.qk, DH1), h3(L.qk2, DH1), rep(gamma_beta[:, 0:DH1], NH, DH1),
                                 ALU.mult).then_inc(L.done, 1)
            for L in lanes:
                e.wait_ge(L.done, before("beta"))
                V_.tensor_tensor(h3(L.qk2, DH1), h3(L.qk, DH1), rep(gamma_beta[:, DH1:2 * DH1], NH, DH1),
                                 ALU.add).then_inc(L.done, 1)
            for w in range(2):
                for L in lanes:
                    e.wait_ge(L.done, before("spread_k%d" % w))
                    V_.tensor_tensor(h3(L.kx[:, w, :], W1N), rep(L.a[:, w * W1N:(w + 1) * W1N], H1, W1N),
                                     bc(head_mask, H1, W1N), ALU.mult).then_inc(L.done, 1)
            for half, heads in enumerate(HALVES):
                for L in lanes:
                    e.wait_ge(L.done, before("maximum%d" % half))
                    V_.tensor_reduce(L.rsum[:, heads], h3(L.pair[half][:, :], W1N), axis=AX.X,
                                     op=ALU.max).then_inc(L.done, 1)
            for half, heads in enumerate(HALVES):
                for L in lanes:
                    e.wait_ge(L.done, before("subtract%d" % half))
                    V_.tensor_tensor(h3(L.s[:, half * UNIT:(half + 1) * UNIT], W1N), h3(L.pair[half][:, :], W1N),
                                     bc(L.rsum[:, heads], H1 // 2, W1N), ALU.subtract).then_inc(L.done, 1)
            for L in lanes:
                e.wait_ge(L.done, before("row_sums"))
                V_.tensor_reduce(L.rsum, h3(L.p, W1N), axis=AX.X, op=ALU.add).then_inc(L.done, 1)
            for L in lanes:
                e.wait_ge(L.done, before("inverse_sums"))
                V_.reciprocal(L.rden, L.rsum).then_inc(L.done, 1)
            for L in lanes:
                e.wait_ge(L.done, before("divide"))
                V_.tensor_tensor(h3(L.o, DH1), h3(L.a[:, 0:P], DH1), bc(L.rden, H1, DH1), ALU.mult).then_inc(L.done, 1)
            for L in lanes:
                e.wait_ge(L.done, before("residual"))
                V_.tensor_tensor(X1[:, tile[L.number], :], L.a[:, 0:P], L.xn, ALU.add).then_inc(L.done, 1)
            layernorm_dve(e, before, tile, lambda L: L.z, "_2")

        def stage1_pool(e, before, tile):
            for L in lanes:
                e.wait_ge(L.done, before("add_bias"))
                G_.tensor_tensor(L.xn, X1[:, tile[L.number], :], bias_out, ALU.add).then_inc(L.done, 1)

        def stage1_act(e, before, tile):
            root_act(e, before, lambda L: L.variance, lambda L: L.scratch, lambda L: L.inverse, "log", "seed")
            for L in lanes:
                e.wait_ge(L.done, before("keep"))
                A_.activation(L.xnT, L.b[:, 0:P], ACT.Copy).then_inc(L.done, 1)
            for L in lanes:
                e.wait_ge(L.done, before("keep_twice"))
                A_.activation(L.twice.rearrange("p (w r t) -> p w r t", w=2, r=2),
                              L.b[:, 0:P].rearrange("p (w o t) -> p w o t", w=2, o=1)
                              .broadcast_to([P, 2, 2, W1N]), ACT.Copy).then_inc(L.done, 1)
            for L in lanes:
                e.wait_ge(L.done, before("squares"))
                A_.activation(L.sq, L.qk, ACT.Square).then_inc(L.done, 1)
            root_act(e, before, lambda L: L.head_var, lambda L: L.head_mean, lambda L: L.head_inv, "head_log", "head_seed")
            for L in lanes:
                e.wait_ge(L.done, before("keep_q"))
                A_.activation(L.qT, L.b[:, 0:P], ACT.Copy).then_inc(L.done, 1)
            for L in lanes:
                e.wait_ge(L.done, before("exp"))
                A_.activation(L.p, L.s, ACT.Exp).then_inc(L.done, 1)
            for half in range(2):
                for L in lanes:
                    e.wait_ge(L.done, before("keep_p%d" % half))
                    A_.activation(L.pt[:, half * UNIT:(half + 1) * UNIT], L.pair[half][:, :],
                                  ACT.Copy).then_inc(L.done, 1)
            for L in lanes:
                e.wait_ge(L.done, before("keep_o"))
                A_.activation(L.oT, L.b[:, 0:P], ACT.Copy).then_inc(L.done, 1)
            root_act(e, before, lambda L: L.variance, lambda L: L.scratch, lambda L: L.inverse, "log_2", "seed_2")
            for L in lanes:
                e.wait_ge(L.done, before("keep_2"))
                A_.activation(xT[:, bass.ds(e.snap(tile[L.number] * P), P)], L.b[:, 0:P], ACT.Copy).then_inc(L.done, 1)

        def stage1_pe(e, before, tile):
            for L in lanes:
                e.wait_ge(L.done, before("transpose"))
                tr(L.b[:, 0:P], L.xn).then_inc(L.done, 1)
            for L in lanes:
                e.wait_ge(L.done, before("project"))
                mm(L.a[:, 0:2 * P], L.xnT, w_qkv[:, 0:2 * P])
                for w in range(2):
                    last = mm(L.b[:, w * P:(w + 1) * P], L.twice[:, w * P:(w + 1) * P], w_qkv[:, 2 * P:3 * P])
                last.then_inc(L.done, 1)
            for L in lanes:
                e.wait_ge(L.done, before("transpose_qk"))
                tr(L.b[:, 0:P], L.qk2[:, 0:P])
                tr(L.a[:, 0:P], L.qk2[:, P:2 * P]).then_inc(L.done, 1)
            for L in lanes:
                e.wait_ge(L.done, before("scores"))
                for w in range(2):
                    for half in range(2):
                        last = mm(L.pair[half][w * W1N:(w + 1) * W1N, :], L.qT[:, w * W1N:(w + 1) * W1N],
                                  L.kx[:, w, half * UNIT:(half + 1) * UNIT])
                last.then_inc(L.done, 1)
            for half in range(2):
                for L in lanes:
                    e.wait_ge(L.done, before("transpose_p%d" % half))
                    for t in range(4):
                        last = tr(L.pair[half][:, t * P:(t + 1) * P], L.p[:, (4 * half + t) * P:(4 * half + t + 1) * P])
                    last.then_inc(L.done, 1)
            for L in lanes:
                e.wait_ge(L.done, before("weigh_values"))
                for t in range(H1 // 2):
                    for w in range(2):
                        last = mm(L.a[w * W1N:(w + 1) * W1N, t * 2 * DH1:(t + 1) * 2 * DH1],
                                  L.pt[:, t * P + w * W1N:t * P + (w + 1) * W1N],
                                  L.v[:, w * P + t * 2 * DH1:w * P + (t + 1) * 2 * DH1])
                last.then_inc(L.done, 1)
            for L in lanes:
                e.wait_ge(L.done, before("transpose_o"))
                tr(L.b[:, 0:P], L.o).then_inc(L.done, 1)
            for L in lanes:
                e.wait_ge(L.done, before("project_out"))
                mm(L.a[:, 0:P], L.oT, w_proj).then_inc(L.done, 1)
            for L in lanes:
                e.wait_ge(L.done, before("transpose_2"))
                tr(L.b[:, 0:P], L.z).then_inc(L.done, 1)

        QUNITS = [(b, u) for b in range(BLOCKS) for u in range(NQK)]
        VUNITS = [(b, v) for b in range(BLOCKS) for v in range(NV)]
        NQ = len(QUNITS)
        ORDER = {0: ("q", 0), 1: ("q", 1), 3: ("q", 2), 4: ("q", 3), 5: ("v", 0), 6: ("q", 4), 7: ("q", 5),
                 8: ("v", 1), 9: ("q", 6), 10: ("q", 7), 11: ("v", 2), 12: ("v", 3)}
        UNITS = list(ORDER.values())
        SEED_STEP = {5: 0, 11: 1}
        NEWTON_STEP = {6: 0, 12: 1}
        SCALE_STEP = {6: (0, 1), 7: (2, 3), 12: (4, 5), 13: (6, 7)}
        T_STEP = {9: (0,), 10: (1,), 11: (2,), 12: (3,), 13: (4,), 14: (5,), 15: (6, 7)}
        T_SIDE = (5, 7)
        SPLIT_STEP = 13
        STEPS = HEADS
        EXP_LAG, T_LAG, KEEP_LAG, PV_LAG = 1, 2, 3, 4
        busy = [n for n in ORDER if ORDER[n][0] == "q"]
        KEPT = {"act": [h for h in range(HEADS) if (h + KEEP_LAG) % STEPS in busy],
                "dve": [h for h in range(HEADS) if (h + KEEP_LAG) % STEPS not in busy]}

        def wait_kept(e, g, h):
            for who, heads in KEPT.items():
                if h % HEADS in heads:
                    e.wait_ge(S["pT_" + who], count("pT_" + who, g, heads.index(h % HEADS) + 1 - (len(heads) if h < 0 else 0)))

        def keep(e, n, g, who, copy):
            h = n - KEEP_LAG
            if 0 <= h < HEADS and h in KEPT[who]:
                e.wait_ge(S["pT_done"], count("pT_done", g, h + 1))
                e.wait_ge(S["pv_done"], count("pv_done", g, h + 1 - NT_))
                copy(PT[:, h % NT_, :], PB[h % 2][:, 0:SW]).then_inc(S["pT_" + who], 1)

        O_STEP = {OH * k + OH - 1 + PV_LAG + 1: k for k in range(OBATCHES)}
        OT_STEP = {n + 2: k for n, k in O_STEP.items()}
        Y_STEP = {STEPS + 7: (0, 1, 2, 3), STEPS + 8: (4, 5, 6, 7)}
        X_STEP = STEPS + 8
        O_IN_PASS = sum(n < STEPS for n in OT_STEP)
        TB_USES = []
        for n in range(STEPS):
            TB_USES += [("last o", OT_STEP[m]) for m in (n + STEPS,) if m in OT_STEP]
            TB_USES += [("y", 0) for m in (n + STEPS,) if m == min(Y_STEP)]
            TB_USES += [("qk", j) for j in T_STEP.get(n, ()) if j not in T_SIDE]
            TB_USES += [("o", OT_STEP[m]) for m in (n,) if m in OT_STEP]

        def tb_free(e, use, g, y, b, a):
            for kind, i in reversed(TB_USES[:TB_USES.index(use)]):
                if kind == "last o" and y:
                    return e.wait_ge(S["oT_kept"], count("oT_kept", g + -1, i + 1))
                if kind == "y" and y:
                    return e.wait_ge(S["x_updated"], count("x_updated", g + -1, 1))
                if kind == "qk" and a:
                    return e.wait_ge(S["qkT_kept"], count("qkT_kept", g + 1, i + 1))
                if kind == "o" and b:
                    return e.wait_ge(S["oT_kept"], count("oT_kept", g, i + 1))
            if b:
                e.wait_ge(S["qkT_kept"], count("qkT_kept", g, NQ))
            elif y:
                e.wait_ge(S["oT_kept"], count("oT_kept", g + -1, O_IN_PASS))

        def t_bank(j):
            return QB[1] if j in T_SIDE else TB

        def a_pe(e, n, g, p, flags):
            if n == 0:
                e.wait_ge(S["xs_ready"], count("xs_ready", g, 1))
            if n in ORDER:
                kind, i = ORDER[n]
                m = UNITS.index((kind, i))
                back = 0 if m >= 2 else 1
                bkind, bi = UNITS[m - 2]
                if bkind == "q":
                    e.wait_ge(S["rotated"], count("rotated", g, bi + 1 - back * NQ))
                else:
                    e.wait_ge(S["v_kept"], count("v_kept", g, bi + 1 - back * len(VUNITS)))
                if m == 1:
                    e.wait_ge(S["qkT_kept"], count("qkT_kept", g, 0))
                b, u = QUNITS[i] if kind == "q" else (VUNITS[i][0], NQK + VUNITS[i][1])
                high, low = (x[:, p, b * P:(b + 1) * P] for x in (xs_h, xs_l))
                cols = slice(u * UNIT, (u + 1) * UNIT)
                bank = QB[m % 2]
                mm(bank[:, :], high, wq_h[:, cols], True, False)
                mm(bank[:, :], low, wq_h[:, cols], False, False)
                mm(bank[:, :], high, wq_l[:, cols], False, True).then_inc(S["qkv_done"], 1)
            for j in T_STEP.get(n, ()):
                e.wait_ge(S["qk_scaled"], count("qk_scaled", g, j + 1))
                if j in T_SIDE:
                    e.wait_ge(S["v_kept"], count("v_kept", g, len(VUNITS)))
                    e.wait_ge(S["qkT_kept"], count("qkT_kept", g, j - 1))
                else:
                    tb_free(e, ("qk", j), g + -1, *flags)
                for t in range(4):
                    last = tr(t_bank(j)[:, t * P:(t + 1) * P], qk[:, j, t * P:(t + 1) * P])
                last.then_inc(S["qkT_done"], 1)

        def a_act(e, n, g, p):
            if n in ORDER:
                kind, i = ORDER[n]
                m = UNITS.index((kind, i))
                e.wait_ge(S["qkv_done"], count("qkv_done", g, m + 1))
                if kind == "q":
                    e.wait_ge(S["summed"], count("summed", g, i - 1))
                    A_.activation(sq[:, i % 2, :], QB[m % 2][:, :], ACT.Square).then_inc(S["squared"], 1)
                else:
                    b, v = VUNITS[i]
                    A_.activation(V[:, p, b, v * UNIT:(v + 1) * UNIT], QB[m % 2][:, :],
                                  ACT.Copy).then_inc(S["v_kept"], 1)
            if n in SEED_STEP:
                b = SEED_STEP[n]
                e.wait_ge(S["guarded"], count("guarded", g, b + 1))
                e.wait_ge(S["normed"], count("normed", g, b))
                A_.activation(rnt[:, :], ss[:, b, :], ACT.Ln, scale=LN_IN_SCALE).then_inc(S["ln_done"], 1)
                e.wait_ge(S["ln_done"], count("ln_done", g, b + 1))
                A_.activation(rn0[:, :], rnt[:, :], ACT.Exp, scale=-0.5,
                              bias=vec_half[:, 0:1]).then_inc(S["seeded"], 1)
            for j in T_STEP.get(n, ()):
                b, u = QUNITS[j]
                e.wait_ge(S["qkT_done"], count("qkT_done", g, j + 1))
                dst = (qT if u < NQK // 2 else kT)[:, p, (u % 2) * 4:(u % 2) * 4 + 4, b * P:(b + 1) * P]
                A_.activation(dst, t_bank(j)[:, :].rearrange("p (t c) -> p t c", t=4),
                              ACT.Copy).then_inc(S["qkT_kept"], 1)

        def a_dve(e, n, g, p):
            if n in ORDER and ORDER[n][0] == "q":
                i = ORDER[n][1]
                m = UNITS.index(ORDER[n])
                b, u = QUNITS[i]
                kind = 0 if u < NQK // 2 else 2
                bank = QB[m % 2]
                e.wait_ge(S["squared"], count("squared", g, i + 1))
                e.wait_ge(S["qk_added"], count("qk_added", g, i - 1))
                V_.tensor_tensor(h3(tc[:, i % 2, :], DH), h3(bank[:, :], DH), rep(tab[:, kind, b, :], UH, DH), ALU.mult)
                halves = dict(a=2, c=DH // 2)
                swapped = bank[:, :].rearrange("p (h a c) -> p h a c", **halves)[:, :, ::-1, :]
                sines = tab[:, kind + 1, b, :].rearrange("p (o a c) -> p o a c", o=1, a=2).broadcast_to([P, UH, 2, DH // 2])
                V_.tensor_tensor(ts[:, i % 2, :].rearrange("p (h a c) -> p h a c", **halves),
                                 swapped, sines, ALU.mult).then_inc(S["rotated"], 1)
                V_.tensor_reduce(ss[:, b, u * UH:(u + 1) * UH], h3(sq[:, i % 2, :], DH), axis=AX.X,
                                 op=ALU.add).then_inc(S["summed"], 1)
                if u == NQK - 1:
                    e.wait_ge(S["summed"], count("summed", g, i + 1))
                    V_.tensor_scalar(ss[:, b, :], ss[:, b, :], 1e-24, None, ALU.max).then_inc(S["guarded"], 1)
            if n in NEWTON_STEP:
                b = NEWTON_STEP[n]
                e.wait_ge(S["seeded"], count("seeded", g, b + 1))
                V_.scalar_tensor_tensor(rnt[:, :], ss[:, b, :], -0.5, rn0[:, :], ALU.mult,
                                        ALU.mult).then_inc(S["newton"], 1)
                e.wait_ge(S["newton"], count("newton", g, 2 * b + 1))
                V_.tensor_tensor(rnt[:, :], rnt[:, :], rn0[:, :], ALU.mult).then_inc(S["newton"], 1)
                e.wait_ge(S["newton"], count("newton", g, 2 * b + 2))
                e.wait_ge(S["qk_scaled"], count("qk_scaled", g, 4 * b + 4 - NQ))
                V_.scalar_tensor_tensor(rn[:, b, :], rnt[:, :], 1.5, rn0[:, :], ALU.add,
                                        ALU.mult).then_inc(S["normed"], 1)

        def a_pool(e, n, g):
            if n in ORDER and ORDER[n][0] == "q":
                i = ORDER[n][1]
                e.wait_ge(S["rotated"], count("rotated", g, i + 1))
                e.wait_ge(S["qkT_done"], count("qkT_done", g, i + 1 - NQ))
                G_.tensor_tensor(qk[:, i, :], tc[:, i % 2, :], ts[:, i % 2, :], ALU.add).then_inc(S["qk_added"], 1)
            for j in SCALE_STEP.get(n, ()):
                b, u = QUNITS[j]
                e.wait_ge(S["normed"], count("normed", g, b + 1))
                e.wait_ge(S["qk_added"], count("qk_added", g, j + 1))
                G_.tensor_tensor(h3(qk[:, j, :], DH), h3(qk[:, j, :], DH),
                                 bc(rn[:, b, u * UH:(u + 1) * UH], UH, DH), ALU.mult).then_inc(S["qk_scaled"], 1)

        def b_pe(e, n, g, p):
            if n < HEADS:
                r = (n % 2) * DH
                if n == 0:
                    e.wait_ge(S["qkT_kept"], count("qkT_kept", g, NQ))
                    e.wait_ge(S["v_kept"], count("v_kept", g, len(VUNITS)))
                e.wait_ge(S["masked"], count("masked", g, n - 1))
                q, k = qT[r:r + DH, p, n // 2, :], kT[r:r + DH, p, n // 2, :]
                mm(SB[n % 2][:, 0:P], q[:, 0:P], k[:, 0:P])
                mm(SB[n % 2][:, P:SW], q[:, P:LEN], k[:, P - WIN:LEN]).then_inc(S["s_done"], 1)

        def b_pe_late(e, n, g, p, flags):
            h = n - T_LAG
            if 0 <= h < HEADS:
                e.wait_ge(S["exp_done"], count("exp_done", g, h + 1))
                wait_kept(e, g, h - 2)
                pr, bank = Pr[:, h % NP_, :], PB[h % 2]
                tr(bank[:, 0:P], pr[:, 0:P])
                tr(bank[:, P:KEYS1], pr[0:WIN, P:2 * P], ident[0:WIN, 0:WIN])
                tr(bank[:, KEYS1:SW], pr[:, 2 * P:3 * P]).then_inc(S["pT_done"], 1)
            h = n - PV_LAG
            if 0 <= h < HEADS:
                wait_kept(e, g, h)
                if h % OH == 0:
                    e.wait_ge(S["o_read"], count("o_read", g, h // OH))
                v = [V[:, p, b, h * DH:(h + 1) * DH] for b in range(BLOCKS)]
                pt = PT[:, h % NT_, :]
                out = [OB[:, (b * OH + h % OH) * DH:(b * OH + h % OH + 1) * DH] for b in range(BLOCKS)]
                mm(out[0], pt[:, 0:P], v[0])
                mm(out[1], pt[:, KEYS1:SW], v[1], True, False, skip_group_check=True)
                mm(out[1][0:WIN, :], pt[:, P:KEYS1], v[0], False, True,
                   skip_group_check=True).then_inc(S["pv_done"], 1)
            if n in OT_STEP:
                k = OT_STEP[n]
                e.wait_ge(S["o_divided"], count("o_divided", g, k + 1))
                if n < STEPS:
                    tb_free(e, ("o", k), g, *flags)
                else:
                    tb_free(e, ("last o", k), g + 1, *flags)
                for j in range(OH // 2):
                    for b in range(BLOCKS):
                        last = tr(TB[:, j * LEN + b * P:j * LEN + (b + 1) * P], osb[:, b, j * P:(j + 1) * P])
                last.then_inc(S["oT_done"], 1)
            for j in Y_STEP.get(n, ()):
                if j == 0:
                    e.wait_ge(S["oT_kept"], count("oT_kept", g, OBATCHES))
                last = mm(TB[:, 0:LEN], wo_sb[:, j, :], oT[:, j, :], j == 0, j == PAIRS - 1, skip_group_check=True)
                if j == PAIRS - 1:
                    last.then_inc(S["y_done"], 1)

        def b_dve(e, n, g, at):
            if n < HEADS:
                e.wait_ge(S["s_done"], count("s_done", g, n + 1))
                e.wait_ge(S["exp_done"], count("exp_done", g, n - 1))
                apart(e)
                for b, (lo, hi) in enumerate(((0, P), (P, SW))):
                    last = V_.tensor_tensor_reduce(
                        out=SM[:, n % 2, lo:hi], in0=SB[n % 2][:, lo:hi], in1=mask[:, lo:hi], scale=1.0,
                        scalar=NEG, op0=ALU.add, op1=ALU.min, accum_out=nmax[:, n, b:b + 1])
                last.then_inc(S["masked"], 1)

            keep(e, n, g, "dve", V_.tensor_copy)
            if n in O_STEP:
                k = O_STEP[n]
                heads = slice(k * OH, (k + 1) * OH)
                e.wait_ge(S["exp_done"], count("exp_done", g, (k + 1) * OH))
                e.wait_ge(S["o_divided"], count("o_divided", g, k - 3))
                V_.reciprocal(rden[:, :, heads], rsum[:, :, heads]).then_inc(S["recip_done"], 1)
            if n == X_STEP:
                e.wait_ge(S["y_done"], count("y_done", g, 1))
                V_.tensor_tensor(xT[:, bass.ds(at, LEN)], TB[:, 0:LEN], xT[:, bass.ds(at, LEN)],
                                 ALU.add).then_inc(S["x_updated"], 1)

        def b_act(e, n, g):
            h = n - EXP_LAG
            if 0 <= h < HEADS:
                e.wait_ge(S["masked"], count("masked", g, h + 1))
                e.wait_ge(S["pT_done"], count("pT_done", g, h + 1 - NP_))
                pr = Pr[:, h % NP_, :]
                A_.activation(pr[:, 0:P], SM[:, h % 2, 0:P], ACT.Exp, scale=-1.0, bias=nmax[:, h, 0:1],
                              accum_out=rsum[:, 0, h:h + 1])
                A_.activation(pr[:, P + ZP:], SM[:, h % 2, P:SW], ACT.Exp, scale=-1.0, bias=nmax[:, h, 1:2],
                              accum_out=rsum[:, 1, h:h + 1]).then_inc(S["exp_done"], 1)
            keep(e, n, g, "act", lambda out, in_: A_.activation(out, in_, ACT.Copy))

        def b_act_late(e, n, g):
            if n in OT_STEP:
                k = OT_STEP[n]
                e.wait_ge(S["oT_done"], count("oT_done", g, k + 1))
                e.wait_ge(S["y_done"], count("y_done", g, 0))
                A_.activation(oT[:, k * OH // 2:(k + 1) * OH // 2, :].rearrange("p j t -> p (j t)"), TB[:, :],
                              ACT.Copy).then_inc(S["oT_kept"], 1)

        def o_act(e, n, g):
            if n in O_STEP:
                k = O_STEP[n]
                e.wait_ge(S["pv_done"], count("pv_done", g, (k + 1) * OH))
                e.wait_ge(S["o_divided"], count("o_divided", g, k))
                A_.activation(oraw[:, :, :].rearrange("p b h -> p (b h)"), OB[:, :], ACT.Copy).then_inc(S["o_read"], 1)

        def o_pool(e, n, g):
            if n in O_STEP:
                k = O_STEP[n]
                heads = slice(k * OH, (k + 1) * OH)
                e.wait_ge(S["recip_done"], count("recip_done", g, k + 1))
                e.wait_ge(S["o_read"], count("o_read", g, k + 1))
                e.wait_ge(S["oT_done"], count("oT_done", g, k))
                G_.tensor_tensor(osb[:, :, :].rearrange("p b (h d) -> p b h d", d=DH),
                                 oraw[:, :, :].rearrange("p b (h d) -> p b h d", d=DH),
                                 rden[:, :, heads].rearrange("p b (h o) -> p b h o", o=1)
                                 .broadcast_to([P, BLOCKS, OH, DH]), ALU.mult).then_inc(S["o_divided"], 1)

        def split_act(e, g, p, at):
            e.wait_ge(S["qkv_done"], count("qkv_done", g, -12))
            A_.activation(xs_h[0:64, p, :], xT[0:64, bass.ds(at, LEN)], ACT.Copy).then_inc(S["xs_hi"], 1)
            A_.activation(xs_h[64:P, p, 1:LEN], xT[64:P, bass.ds(at, LEN - 1)], ACT.Copy).then_inc(S["xs_hi"], 1)

        def split_dve(e, g, p, at):
            e.wait_ge(S["xs_hi"], count("xs_hi", g, 2))
            V_.tensor_tensor(xs_l[0:64, p, :], xT[0:64, bass.ds(at, LEN)],
                             xs_h[0:64, p, :].bitcast(F32), ALU.subtract)
            V_.tensor_tensor(xs_l[64:P, p, 1:LEN], xT[64:P, bass.ds(at, LEN - 1)],
                             xs_h[64:P, p, 1:LEN].bitcast(F32), ALU.subtract).then_inc(S["xs_ready"], 1)

        def pass_pe(e, g, p, at, y, b, a, x):
            flags = (y, b, a)
            for n in range(STEPS):
                if b:
                    b_pe(e, n, g, p)
                if y:
                    b_pe_late(e, n + STEPS, g + -1, 1 - p, flags)
                if a:
                    a_pe(e, n, g + 1, 1 - p, flags)
                if b:
                    b_pe_late(e, n, g, p, flags)

        def pass_act(e, g, p, at, y, b, a, x):
            for n in range(STEPS):
                if y:
                    b_act(e, n + STEPS, g + -1)
                    o_act(e, n + STEPS, g + -1)
                if b:
                    o_act(e, n, g)
                    b_act(e, n, g)
                if a:
                    a_act(e, n, g + 1, 1 - p)
                if x and n == SPLIT_STEP:
                    split_act(e, g + 2, p, at + 2 * LEN)
                if y:
                    b_act_late(e, n + STEPS, g + -1)
                if b:
                    b_act_late(e, n, g)

        def pass_dve(e, g, p, at, y, b, a, x):
            for n in range(STEPS):
                if y:
                    b_dve(e, n + STEPS, g + -1, at - LEN)
                if b:
                    b_dve(e, n, g, at)
                if a:
                    a_dve(e, n, g + 1, 1 - p)
                if x and n == SPLIT_STEP:
                    split_dve(e, g + 2, p, at + 2 * LEN)

        def pass_pool(e, g, p, at, y, b, a, x):
            for n in range(STEPS):
                if y:
                    o_pool(e, n + STEPS, g + -1)
                if b:
                    o_pool(e, n, g)
                if a:
                    a_pool(e, n, g + 1)

        def attention(e, layer, one_pass, split):
            first = Pass(e, e.snap(layer * SEQS))
            if split:
                split(e, first, 0, 0)
            one_pass(e, first + -1, 1, -LEN, False, False, True, True)
            one_pass(e, first, 0, 0, False, True, True, True)
            with e.Fori(0, SEQS // 2 - 2) as i:
                g = Pass(e, e.snap(layer * SEQS + i * 2))
                at = e.snap(i * (2 * LEN))
                one_pass(e, g + 1, 1, at + LEN, True, True, True, True)
                one_pass(e, g + 2, 0, at + 2 * LEN, True, True, True, True)
            for n in range(SEQS - 3, SEQS + 1):
                one_pass(e, first + n, n % 2, n * LEN, True, n < SEQS, n < SEQS - 1, n < SEQS - 2)

        FT1, FT2, FY, FW = banks[0:2], banks[0], banks[1], banks[2:8]
        NT = GROUP // P
        xf = qk[:, 0:2, :]
        tok = flat(V[:, :, :, :])
        xn = oT[:, 0:4, :].rearrange("p (s j) t -> p s (j t)", s=2)
        xnf = qk[:, 2:4, :]
        f_h, f_l = (x[:, 0:2 * GROUP].rearrange("p (s t) -> p s t", s=2) for x in (wq_h, wq_l))
        gate = qk[:, 4:7, :]
        hid = [[sq[:, 0, :], sq[:, 1, :], tc[:, 0, :]], [tc[:, 1, :], ts[:, 1, :], qk[:, 7, :]]]
        f_st = ts[:, 0, 0:6 * TILES]
        f_mv = ts[:, 0, 192:192 + 2 * TILES].rearrange("p (t c) -> p t c", c=2)
        f_v, f_y, f_t, f_i = (ts[:, 0, 256 + TILES * k:256 + TILES * (k + 1)] for k in range(4))
        F_ORDER = [(j, k) for j in range(3) for k in (1, 0)]

        def f_shift_dve(e, g, i, p):
            at = i * GROUP
            e.wait_ge(S["f_t1"], count("f_t1", g, -1))
            two = dict(a=2, c=LEN)
            V_.tensor_copy(xf[0:64, p, :], xT[0:64, at:at + GROUP])
            V_.tensor_copy(xf[64:P, p, :].rearrange("p (a c) -> p a c", **two)[:, :, 1:],
                           xT[64:P, at:at + GROUP].rearrange("p (a c) -> p a c", **two)[:, :, 0:LEN - 1]
                           ).then_inc(S["f_shifted"], 1)

        def f_rows_pe(e, g, i, p):
            e.wait_ge(S["f_shifted"], count("f_shifted", g, 1))
            e.wait_ge(S["f_tok"], count("f_tok", g, -1))
            for t in range(NT):
                last = tr(FT1[p][:, t * P:(t + 1) * P], xf[:, p, t * P:(t + 1) * P])
            last.then_inc(S["f_t1"], 1)

        def f_rows_act(e, g, i, p):
            e.wait_ge(S["f_t1"], count("f_t1", g, 1))
            A_.activation(tok[:, i * GROUP:(i + 1) * GROUP], FT1[p][:, :], ACT.Copy).then_inc(S["f_tok"], 1)

        def f_rows_dve(e, g, i, p):
            if i == 0:
                f_shift_dve(e, g, i, p)
            if i + 1 < GROUPS:
                f_shift_dve(e, g + 1, i + 1, 1 - p)
            e.wait_ge(S["f_tok"], count("f_tok", g, 1))
            apart(e)
            for t in range(NT):
                V_.bn_stats(f_st[:, 6 * (i * NT + t):6 * (i * NT + t + 1)],
                            tok[:, (i * NT + t) * P:(i * NT + t + 1) * P]).then_inc(S["f_stats"], 1)

        def f_deviation_dve(e, layer):
            g = Pass(e, e.snap(layer * 1))
            e.wait_ge(S["f_stats"], count("f_stats", Pass(e, e.snap(layer * GROUPS), GROUPS - 1), NT))
            apart(e)
            for t in range(TILES):
                last = V_.bn_aggr(f_mv[:, t, :], f_st[:, 6 * t:6 * t + 6])
            n = 0

            def chain(ins):
                nonlocal n
                n += 1
                ins.then_inc(S["f_chain"], 1)
                e.wait_ge(S["f_chain"], count("f_chain", g, n))

            chain(last)
            chain(V_.tensor_scalar(f_v, f_mv[:, :, 1], LN_EPS, None, ALU.add))
            chain(V_.tensor_scalar(f_i.bitcast(I32), f_v.bitcast(I32), 1, None, ALU.logical_shift_right))
            chain(V_.tensor_scalar(f_y.bitcast(I32), f_i.bitcast(I32), -1.0, 1597463007.0, ALU.mult, ALU.add))
            for _ in range(3):
                chain(V_.scalar_tensor_tensor(f_t, f_v, -0.5, f_y, ALU.mult, ALU.mult))
                chain(V_.tensor_tensor(f_t, f_t, f_y, ALU.mult))
                chain(V_.scalar_tensor_tensor(f_y, f_t, 1.5, f_y, ALU.add, ALU.mult))
            assert n == COUNTS["f_chain"][0], n

        def f_norm_dve(e, g, i, p):
            e.wait_ge(S["f_t2"], count("f_t2", g, -1))
            for t in range(NT):
                row = i * NT + t
                at = tok[:, (i * NT + t) * P:(i * NT + t + 1) * P]
                last = V_.tensor_scalar(xn[:, p, t * P:(t + 1) * P], at, f_mv[:, row, 0:1], f_y[:, row:row + 1],
                                        ALU.subtract, ALU.mult)
            last.then_inc(S["f_normed"], 1)

        def f_t2_pe(e, g, i, p):
            e.wait_ge(S["f_normed"], count("f_normed", g, 1))
            e.wait_ge(S["f_xn"], count("f_xn", g, 0))
            for t in range(NT):
                last = tr(FT2[:, t * P:(t + 1) * P], xn[:, p, t * P:(t + 1) * P])
            last.then_inc(S["f_t2"], 1)

        def f_scale_act(e, g, i, p):
            e.wait_ge(S["f_t2"], count("f_t2", g, 1))
            e.wait_ge(S["f_split"], count("f_split", g, -1))
            A_.activation(xnf[:, p, :], FT2[:, :], ACT.Identity, scale=vec[:, 0:1],
                          bias=vec[:, 1:2]).then_inc(S["f_xn"], 1)
            e.wait_ge(S["f_xn"], count("f_xn", g, 1))
            e.wait_ge(S["f_w1"], count("f_w1", g, -6))
            A_.activation(f_h[:, p, :], xnf[:, p, :], ACT.Copy).then_inc(S["f_hi"], 1)

        def f_split_pool(e, g, i, p):
            e.wait_ge(S["f_hi"], count("f_hi", g, 1))
            G_.tensor_tensor(f_l[:, p, :], xnf[:, p, :], f_h[:, p, :].bitcast(F32),
                             ALU.subtract).then_inc(S["f_split"], 1)

        def f_w1_pe(e, g, i, p):
            h, l = f_h[:, p, :], f_l[:, p, :]
            e.wait_ge(S["f_split"], count("f_split", g, 1))
            for m, (j, k) in enumerate(F_ORDER):
                lo, size = HTILE[j]
                e.wait_ge(S["f_gelu" if k else "f_gated"], count("f_gelu" if k else "f_gated", g, j - 2))
                c = slice(k * HID + lo, k * HID + lo + size)
                mm(FW[m][0:size, :], w1_h[:, c], h, True, False)
                mm(FW[m][0:size, :], w1_l[:, c], h, False, False)
                mm(FW[m][0:size, :], w1_h[:, c], l, False, True).then_inc(S["f_w1"], 1)

        def f_gelu_act(e, g, i, p):
            for j, (lo, size) in enumerate(HTILE):
                e.wait_ge(S["f_w1"], count("f_w1", g, 2 * j + 1))
                e.wait_ge(S["f_gated"], count("f_gated", g, j - 2))
                A_.activation(gate[0:size, j, :], FW[2 * j][0:size, :], ACT.Gelu,
                              bias=vec[0:size, 5 + j:6 + j]).then_inc(S["f_gelu"], 1)

        def f_gate_dve(e, g, i, p):
            for j, (lo, size) in enumerate(HTILE):
                e.wait_ge(S["f_w1"], count("f_w1", g, 2 * j + 2))
                e.wait_ge(S["f_gelu"], count("f_gelu", g, j + 1))
                if j == 0:
                    e.wait_ge(S["f_w2"], count("f_w2", g, -1))
                V_.scalar_tensor_tensor(hid[p][j][0:size, :], FW[2 * j + 1][0:size, :], vec[0:size, 2 + j:3 + j],
                                        gate[0:size, j, :], ALU.add, ALU.mult).then_inc(S["f_gated"], 1)

        def f_w2_pe(e, g, i, p):
            e.wait_ge(S["f_x"], count("f_x", g, 0))
            for j, (lo, size) in enumerate(HTILE):
                e.wait_ge(S["f_gated"], count("f_gated", g, j + 1))
                last = mm(FY[:, :], w2_sb[0:size, j, :], hid[p][j][0:size, :], j == 0, j == 2)
            last.then_inc(S["f_w2"], 1)

        def f_x_dve(e, g, i, p):
            at = i * GROUP
            e.wait_ge(S["f_w2"], count("f_w2", g, 1))
            V_.scalar_tensor_tensor(xT[:, at:at + GROUP], FY[:, :], vec[:, 8:9], xT[:, at:at + GROUP],
                                    ALU.add, ALU.add).then_inc(S["f_x"], 1)

        F_PASS = {"pe": ((f_t2_pe, 1), (f_w1_pe, 0), (f_w2_pe, -1)),
                  "act": ((f_scale_act, 1), (f_gelu_act, 0)),
                  "dve": ((f_norm_dve, 2), (f_gate_dve, 0), (f_x_dve, -1)),
                  "pool": ((f_split_pool, 1),)}

        def feed_forward(e, layer, who):
            rows = {"pe": f_rows_pe, "act": f_rows_act, "dve": f_rows_dve}.get(who)
            first = Pass(e, e.snap(layer * GROUPS))
            if who == "act":
                prepare_ffn_act(e, layer)
            if who == "dve":
                for p in range(2):
                    V_.memset(xf[64:P, p, :].rearrange("p (a c) -> p a c", a=2)[:, :, 0:1], 0.0)
            if rows:
                for i in range(GROUPS):
                    rows(e, first + i, i, i % 2)
            if who == "dve":
                f_deviation_dve(e, layer)
            if who == "pool":
                prepare_ffn_pool(e, layer)
            if who == "pe":
                e.wait_ge(S["w1_ready"], layer + 1)

            for n in range(-2, GROUPS + 1):
                for stage, ahead in F_PASS[who]:
                    i = n + ahead
                    if 0 <= i < GROUPS:
                        stage(e, first + i, i, i % 2)

        C3 = 3 * INNER
        CA = C3 // 2

        def prepare_act(e, layer):
            A_.preload_act_table_set("natural_log_exp_and_others")
            e.wait_ge(S["attn_loaded"], layer * 48 + 48)
            A_.activation(wq_h[:, 0:CA], wq_raw[:, 0:CA], ACT.Copy).then_inc(S["prep"], 1)
            A_.activation(wq_h[:, CA:], wq_raw[:, CA:], ACT.Copy).then_inc(S["prep"], 1)

        def prepare_dve(e, layer):
            for x in (xs_h, xs_l):
                V_.memset(x[64:P, :, 0:1].bitcast(F32), 0.0)
            e.wait_ge(S["attn_loaded"], layer * 48 + 48)
            swapped = [qks[:, i, :].rearrange("p (o a c) -> p o a c", o=1, a=2)[:, :, ::-1, :]
                       .broadcast_to([P, BLOCKS, 2, DH // 2]) for i in range(2)]
            for i in range(2):
                V_.tensor_tensor(tab[:, 2 * i, :, :], rot[:, 2 * i, :, :], rep(qks[:, i, :], BLOCKS, DH), ALU.mult)
                V_.tensor_tensor(tab[:, 2 * i + 1, :, :].rearrange("p b (a c) -> p b a c", a=2),
                                 rot[:, 2 * i + 1, :, :].rearrange("p b (a c) -> p b a c", a=2), swapped[i], ALU.mult)
            e.wait_ge(S["prep"], layer * 2 + 1)
            V_.tensor_tensor(wq_l[:, 0:CA], wq_raw[:, 0:CA], wq_h[:, 0:CA].bitcast(F32), ALU.subtract)

        def prepare_pool(e, layer):
            e.wait_ge(S["prep"], layer * 2 + 2)
            G_.tensor_tensor(wq_l[:, CA:], wq_raw[:, CA:], wq_h[:, CA:].bitcast(F32), ALU.subtract)

        def prepare_ffn_act(e, layer):
            e.wait_ge(S["ffn_loaded"], layer * 48 + 48)
            A_.activation(w1_h[:, :], w1_raw[:, :], ACT.Copy).then_inc(S["prep_ffn"], 1)

        def prepare_ffn_pool(e, layer):
            e.wait_ge(S["prep_ffn"], layer + 1)
            G_.tensor_tensor(w1_l[:, :], w1_raw[:, :], w1_h[:, :].bitcast(F32), ALU.subtract).then_inc(S["w1_ready"], 1)

        o_in = qk[:, 0, :]
        o_out = qk[:, 1:3, :]

        def finish(e, who):
            with e.Fori(0, GROUPS) as i:
                if who == "act":
                    e.wait_ge(S["o_t"], i + 1)
                    A_.activation(o_in, xT[:, bass.ds(i * GROUP, GROUP)], ACT.Copy).then_inc(S["o_copied"], 1)
                if who == "pe":
                    e.wait_ge(S["o_copied"], i + 1)
                    e.wait_ge(S["o_sum"], i + 1)
                    for t in range(NT):
                        last = tr(FT1[0][:, t * P:(t + 1) * P], o_in[:, t * P:(t + 1) * P])
                    last.then_inc(S["o_t"], 1)
                if who == "dve":
                    e.wait_ge(S["o_t"], i + 2)
                    V_.tensor_tensor(X1[:, bass.ds(i * NT, NT), :], X1[:, bass.ds(i * NT, NT), :],
                                     h3(FT1[0][:, :], P), ALU.add).then_inc(S["o_sum"], 1)

        def program(e, who, one_pass, split, prepare):
            stage1(e, {"pe": stage1_pe, "act": stage1_act, "dve": stage1_dve, "pool": stage1_pool}[who])
            meet(e, 1)
            with e.Fori(0, DEPTH) as layer:
                if prepare:
                    prepare(e, layer)
                meet(e, layer * MEETINGS + 2)
                attention(e, layer, one_pass, split)
                meet(e, layer * MEETINGS + 3)
                feed_forward(e, layer, who)
                meet(e, layer * MEETINGS + 4)
            finish(e, who)

        @block.sync
        def _(sp):
            for dst, src in ((X1[:, :, :], x_in.rearrange("(t p) d -> p t d", p=P)), (small[:, :], c_small),
                             (w1_raw[:, 0:w_first.shape[1]], w_first),
                             (rot[:, :, :, :].rearrange("p a b c -> p (a b c)"), c_rot)):
                sp.dma_start(dst, src).then_inc(S["loaded"], 16)
            with sp.Fori(0, DEPTH) as layer:
                sp.wait_ge(S["phase"], layer * (MEETINGS * ENGINES) + (3 - MEETINGS) * ENGINES + PHASE_AHEAD)
                sp.dma_start(wq_raw[:, :], wqkv[layer, :, :]).then_inc(S["attn_loaded"], 16)
                sp.dma_start(wo_sb[:, :, :].rearrange("p a b -> p (a b)"), wo[layer, :, :]).then_inc(S["attn_loaded"], 16)
                sp.dma_start(qks[:, :, :].rearrange("p a b -> p (a b)"), qkscale[layer, :, :]).then_inc(S["attn_loaded"], 16)
                sp.wait_ge(S["phase"], layer * (MEETINGS * ENGINES) + ENGINES + PHASE_AHEAD)
                sp.dma_start(w1_raw[:, :], fw1[layer, :, :]).then_inc(S["ffn_loaded"], 16)
                sp.dma_start(w2_sb[:, :, :].rearrange("p a b -> p (a b)"), fw2[layer, :, :]).then_inc(S["ffn_loaded"], 16)
                sp.dma_start(vec[:, :], vectors[layer, :, :]).then_inc(S["ffn_loaded"], 16)
            o = out.rearrange("(t p) d -> p t d", p=P)
            for i in range(GROUPS):
                sp.wait_ge(S["o_sum"], i + 2)
                sp.dma_start(o[:, i * NT:(i + 1) * NT, :], X1[:, i * NT:(i + 1) * NT, :]).then_inc(S["stored"], 16)
            sp.wait_ge(S["stored"], 16 * GROUPS)

        @block.gpsimd
        def _(pool):
            give_ahead(pool)
            pool.wait_ge(S["loaded"], 64)
            G_.memset(Pr[:, :, :], 0.0).then_inc(S["zeroed"], 1)
            G_.memset(vec_half[:, :], HALF_LOG).then_inc(S["zeroed"], 1)
            program(pool, "pool", pass_pool, None, prepare_pool)

        @block.scalar
        def _(act):
            act.wait_ge(S["loaded"], 64)
            act.wait_ge(S["zeroed"], 2)
            A_.preload_act_table_set("natural_log_exp_and_others")
            program(act, "act", pass_act, split_act, prepare_act)

        @block.vector
        def _(dve):
            dve.wait_ge(S["loaded"], 64)
            program(dve, "dve", pass_dve, split_dve, prepare_dve)

        @block.tensor
        def _(pe):
            pe.wait_ge(S["loaded"], 64)
            program(pe, "pe", pass_pe, None, None)


def kernel(L0_attn_x, L0_attn_W_qkv, L0_attn_ln_gamma, L0_attn_ln_beta, L0_attn_W_proj, L0_attn_b_proj, L0_ffn_Wqkv,
           L0_ffn_q_scale, L0_ffn_k_scale, L0_ffn_Wo, L0_ffn_ln_g, L0_ffn_ln_b, L0_ffn_W1, L0_ffn_b1, L0_ffn_W2,
           L0_ffn_b2):
    import concourse.bacc as bacc
    from concourse.bass_utils import run_bass_kernel_spmd

    a = lambda x: np.ascontiguousarray(x)
    wide = lambda x: np.broadcast_to(a(x)[None, :], (P, x.shape[0]))
    first = np.concatenate([a(L0_attn_W_qkv), a(L0_attn_W_proj), wide(L0_attn_b_proj), wide(L0_attn_ln_gamma),
                            wide(L0_attn_ln_beta)], 1)
    scales = np.stack([a(L0_ffn_q_scale), a(L0_ffn_k_scale)], 1).reshape(DEPTH, 1, 2 * DH)
    w2 = np.zeros((DEPTH, 3 * P, DM), np.float32)
    w2[:, :HID] = a(L0_ffn_W2)
    vectors = np.zeros((DEPTH, P, 9), np.float32)
    vectors[:, :, 0], vectors[:, :, 1], vectors[:, :, 8] = a(L0_ffn_ln_g), a(L0_ffn_ln_b), a(L0_ffn_b2)
    for k in range(2):
        for j, (lo, size) in enumerate(HTILE):
            vectors[:, :size, 2 + 3 * k + j] = a(L0_ffn_b1)[:, k * HID + lo:k * HID + lo + size]
    c_rot, c_small = consts()
    arrays = {
        "x_in": a(L0_attn_x).reshape(TOKENS, DM),
        "w_first": first,
        "wqkv": a(L0_ffn_Wqkv),
        "wo": a(L0_ffn_Wo).reshape(DEPTH, PAIRS, P, DM).transpose(0, 2, 1, 3).reshape(DEPTH, P, PAIRS * DM),
        "qkscale": np.broadcast_to(scales, (DEPTH, P, 2 * DH)),
        "fw1": a(L0_ffn_W1),
        "fw2": w2.reshape(DEPTH, 3, P, DM).transpose(0, 2, 1, 3).reshape(DEPTH, P, 3 * DM),
        "vectors": vectors,
        "c_rot": c_rot,
        "c_small": c_small,
    }
    arrays = {k: np.ascontiguousarray(v) for k, v in arrays.items()}
    nc = bacc.Bacc("TRN2", target_bir_lowering=False, num_devices=1)
    args = [nc.dram_tensor(k, v.shape, mybir.dt.from_np(v.dtype), kind="ExternalInput").ap() for k, v in arrays.items()]
    out = nc.dram_tensor("out", (TOKENS, DM), F32, kind="ExternalOutput").ap()
    build(nc, *args, out)
    r = run_bass_kernel_spmd(nc, [arrays], core_ids=[0])
    return r.results[0]["out"].reshape(SEQS, LEN, DM)
```
